# Optimizing a Trainium2 kernel written in Bass

```python
import numpy as np
import jax
import jax.numpy as jnp

def _softmax(x, axis=-1):
    return jax.nn.softmax(x, axis=axis)

def _gelu(x):
    return jax.nn.gelu(x, approximate=True)

def _silu(x):
    return jax.nn.silu(x)

def _sigmoid(x):
    return jax.nn.sigmoid(x)

def _layernorm(x, axis=-1, eps=1e-05):
    m = jnp.mean(x, axis=axis, keepdims=True)
    v = jnp.var(x, axis=axis, keepdims=True)
    return (x - m) / jnp.sqrt(v + eps)

def _scatter_add(tgt, idx, src, axis=0):
    return tgt.at[idx].add(src)

def _segment_sum(src, seg, n):
    return jax.ops.segment_sum(src, seg, n)
kernel_name = 'mk_seq_postln_d1_jaxref_r8_9c6664'

def setup_inputs(seed: int=0):
    np.random.seed(seed)
    _w = jnp.asarray

    def _L0_attn_setup():
        import jax, jax.numpy as jnp
        import numpy as np
        DIM = 128
        key = jax.random.key(seed)
        kx, kw = jax.random.split(key)
        x = jax.random.normal(kx, (4, 256, DIM), dtype=jnp.float32)
        W_qkv = jax.random.normal(kw, (3 * DIM, DIM), dtype=jnp.float32) * DIM ** (-0.5)
        return {'x': x, 'W_qkv': W_qkv}
    _L0_attn_in = _L0_attn_setup()

    def _L0_ffn_setup():
        import jax, jax.numpy as jnp
        import numpy as np
        E, K, D, H = (8, 2, 128, 256)
        B, S = (1, 128)

        def _grouped_swiglu(x_sorted, counts, w1, w2, w3):
            if hasattr(jax.lax, 'ragged_dot'):
                gs = counts.astype(jnp.int32)
                h = jax.nn.silu(jax.lax.ragged_dot(x_sorted, w1, gs)) * jax.lax.ragged_dot(x_sorted, w3, gs)
                return jax.lax.ragged_dot(h, w2, gs)
            pos = jnp.arange(x_sorted.shape[0])
            eid = jnp.searchsorted(jnp.cumsum(counts), pos, side='right')
            out = jnp.zeros((x_sorted.shape[0], w2.shape[-1]), x_sorted.dtype)
            for e in range(w1.shape[0]):
                xm = jnp.where((eid == e)[:, None], x_sorted, 0.0)
                he = jax.nn.silu(xm @ w1[e]) * (xm @ w3[e])
                out = out + he @ w2[e]
            return out
        key = jax.random.key(seed)
        k0, k1, k2, k3, k4 = jax.random.split(key, 5)
        sD = 1.0 / np.sqrt(D)
        sH = 1.0 / np.sqrt(H)
        return {'hidden_states': jax.random.normal(k0, (B, S, D), jnp.float32), 'gate_w': jax.random.normal(k1, (E, D), jnp.float32) * sD, 'w1': jax.random.normal(k2, (E, D, H), jnp.float32) * sD, 'w2': jax.random.normal(k3, (E, H, D), jnp.float32) * sH, 'w3': jax.random.normal(k4, (E, D, H), jnp.float32) * sD}
    _L0_ffn_in = _L0_ffn_setup()
    _d = {'L0_attn_x': _L0_attn_in['x'], 'L0_attn_W_qkv': _L0_attn_in['W_qkv'], 'L0_ffn_gate_w': _L0_ffn_in['gate_w'], 'L0_ffn_w1': _L0_ffn_in['w1'], 'L0_ffn_w2': _L0_ffn_in['w2'], 'L0_ffn_w3': _L0_ffn_in['w3']}
    _x0 = _d['L0_attn_x']
    _d['L0_attn_x'] = jax.random.normal(jax.random.fold_in(jax.random.key(seed), 1), (32, 256, 128), dtype=_x0.dtype)
    del _x0
    return _d

def reference(L0_attn_x, L0_attn_W_qkv, L0_ffn_gate_w, L0_ffn_w1, L0_ffn_w2, L0_ffn_w3):

    def _L0_attn_ref(x, W_qkv):
        import jax, jax.numpy as jnp
        import numpy as np
        DIM = 128
        qkv = jnp.einsum('bnd,ed->bne', x, W_qkv)
        B, N, _ = qkv.shape
        qkv = qkv.reshape(B, N, 3, DIM).transpose(2, 0, 1, 3)
        q, k, v = (qkv[0], qkv[1], qkv[2])
        scale = DIM ** (-0.5)
        attn = jnp.einsum('bnd,bmd->bnm', q * scale, k)
        attn = jax.nn.softmax(attn, axis=-1)
        out = jnp.einsum('bnm,bmd->bnd', attn, v)
        return out

    def _L0_ffn_ref(hidden_states, gate_w, w1, w2, w3):
        import jax, jax.numpy as jnp
        import numpy as np
        E, K, D, H = (8, 2, 128, 256)
        B, S = (1, 128)

        def _grouped_swiglu(x_sorted, counts, w1, w2, w3):
            if hasattr(jax.lax, 'ragged_dot'):
                gs = counts.astype(jnp.int32)
                h = jax.nn.silu(jax.lax.ragged_dot(x_sorted, w1, gs)) * jax.lax.ragged_dot(x_sorted, w3, gs)
                return jax.lax.ragged_dot(h, w2, gs)
            pos = jnp.arange(x_sorted.shape[0])
            eid = jnp.searchsorted(jnp.cumsum(counts), pos, side='right')
            out = jnp.zeros((x_sorted.shape[0], w2.shape[-1]), x_sorted.dtype)
            for e in range(w1.shape[0]):
                xm = jnp.where((eid == e)[:, None], x_sorted, 0.0)
                he = jax.nn.silu(xm @ w1[e]) * (xm @ w3[e])
                out = out + he @ w2[e]
            return out
        x = hidden_states.reshape(-1, D)
        N = x.shape[0]
        scores = jax.nn.softmax(x @ gate_w.T, axis=-1)
        top_scores, sel = jax.lax.top_k(scores, K)
        sel_flat = sel.T.reshape(-1)
        scores_flat = top_scores.T.reshape(-1)
        order = jnp.argsort(sel_flat, stable=True)
        tok_sorted = order % N
        scores_sorted = scores_flat[order]
        counts = jnp.bincount(sel_flat, length=E)
        x_sorted = x[tok_sorted]
        y = _grouped_swiglu(x_sorted, counts, w1, w2, w3)
        weighted = y * scores_sorted[:, None]
        out = jnp.zeros((N, D), x.dtype).at[tok_sorted].add(weighted)
        return out.reshape(hidden_states.shape)
    x = L0_attn_x
    x = _layernorm(x + _L0_attn_ref(x, L0_attn_W_qkv), axis=-1)
    x = _layernorm(x + _L0_ffn_ref(x, L0_ffn_gate_w, L0_ffn_w1, L0_ffn_w2, L0_ffn_w3), axis=-1)
    return x

_drawn_inputs = setup_inputs


def setup_inputs(seed=0):
    import zlib

    import numpy as np

    out = dict(_drawn_inputs(seed))
    spreads = {}
    factors = {}
    for name, (base, spread) in spreads.items():
        noise = np.random.default_rng([zlib.crc32(name.encode()), seed]).standard_normal(out[name].shape)
        drawn = base * np.exp(spread * noise) if base else spread * noise
        out[name] = jnp.asarray(drawn.astype(out[name].dtype))
    for name, factor in factors.items():
        out[name] = (out[name] * factor).astype(out[name].dtype)
    return out
```

```python
from contextlib import ExitStack

import concourse.bass as bass
from concourse import mybir

F32 = mybir.dt.float32
BF16 = mybir.dt.bfloat16
I32 = mybir.dt.int32
U32 = mybir.dt.uint32
ALU = mybir.AluOpType
ACT = mybir.ActivationFunctionType
X = mybir.AxisListType.X

P = 128
EPS = 1e-5


class At:

    def __init__(self, quarter, offset):
        self.quarter, self.offset = quarter, offset

    def __add__(self, n):
        return At(self.quarter, self.offset + n)

    def __sub__(self, n):
        return At(self.quarter, self.offset - n)

    @property
    def number(self):
        return self.quarter * 4 + self.offset

    @property
    def slot(self):
        return self.offset % 4

    @property
    def half(self):
        return self.offset % 2

    @property
    def turn(self):
        return self.quarter + self.offset // 4

    def valid(self, count):
        return not isinstance(self.quarter, int) or 0 <= self.number < count


def wait(engine, semaphore, value):
    if not isinstance(value, int) or value > 0:
        engine.wait_ge(semaphore, value)


def steps(engine, first_whole, last_whole, last, step):
    turns = (last_whole + 1 - first_whole) // 4
    for n in range(first_whole):
        step(At(0, n))
    with engine.Fori(0, turns) as turn:
        for n in range(4):
            step(At(turn, first_whole + n))
    for n in range(first_whole + 4 * turns, last + 1):
        step(At(0, n))


def attention_moe(nc, x, w_qkv, gate_w, w1, w2, w3, out):
    BATCHES, N, D = x.shape
    E, _, H = w1.shape
    C = N // P
    TILES = BATCHES * C
    TOKENS = BATCHES * N
    K = 2
    HC = H // P
    REGION = TOKENS + P
    DUMMY = E * REGION
    BLOCKS = -(-(TOKENS * K // P + E - 1) // 4) * 4
    ROW = D + 2
    SKIP = 2 * TOKENS
    SCALE = float(D) ** -0.5
    GROUP = 4
    GROUPS = TILES // GROUP
    assert D == P and N == 2 * P and H == 2 * P and BATCHES % 4 == 0

    x_tiles = x.rearrange("b (c p) d -> b p c d", p=P)
    out_groups = out.rearrange("b (c p) d -> p (b c) d", p=P)
    rows_dram = nc.dram_tensor("expert_rows", [DUMMY + P, ROW], F32, kind="Internal").ap()
    y_dram = nc.dram_tensor("expert_outputs", [2 * TOKENS, D], F32, kind="Internal").ap()
    y_groups = y_dram.rearrange("(t p k) d -> p t (k d)", p=P, k=K)

    with ExitStack() as ctx:
        def sb(name, shape, dt=F32):
            return ctx.enter_context(nc.sbuf_tensor(name, shape, dt))

        def sem(name):
            return ctx.enter_context(nc.semaphore(name))

        def sems(name, n):
            return [sem(f"{name}{i}") for i in range(n)]

        ident = sb("ident", [P, P])
        before = sb("before", [P, P], BF16)
        ones = sb("ones", [P, P], BF16)
        lane_i = sb("lane_i", [P, 8], I32)
        lane_f = sb("lane_f", [P, E])
        region_f = sb("region_f", [P, E])
        block_i = sb("block_i", [P, BLOCKS], I32)
        block_f = sb("block_f", [P, BLOCKS])
        token_i = sb("token_i", [P, TILES], I32)
        token_f = sb("token_f", [P, TILES])
        padding = sb("padding", [P, ROW])
        w_in = sb("w_in", [P, 3, D])
        wqk = sb("wqk", [P, D])
        wvT = sb("wvT", [P, D])
        gate_in = sb("gate_in", [E, D])
        gateT = sb("gateT", [P, E])
        w13 = sb("w13", [P, E, 2, H])
        w2s = sb("w2s", [P, E, HC, D])

        eps_col = sb("eps_col", [P, 1])

        xin = sb("xin", [P, 4, C, D])
        xT = sb("xT", [P, 2, N])
        yv = sb("yv", [P, 2, 2, N])
        nmax = sb("nmax", [P, 2, C])
        prob = sb("prob", [P, 2, C, N])
        psum_ = sb("psum_", [P, 2, C])
        rinv = sb("rinv", [P, 2, C])
        probT = sb("probT", [P, 2, C, N])
        hid = sb("hid", [P, 2, C, D])
        stats = sb("stats", [P, C, 6])
        mv = sb("mv", [P, 2, C, 2])
        lnv = sb("lnv", [P, C, 1])
        rstd = sb("rstd", [P, 2, C])
        x1 = sb("x1", [P, 4, C, ROW])
        x1T = sb("x1T", [P, 2, N])
        top = sb("top", [P, 2, C, 8])
        best = sb("best", [P, 2, C, 8], U32)
        onehot = sb("onehot", [P, 2, C, K, E])
        chosen = sb("chosen", [P, 2, C, E], BF16)
        seen = sb("seen", [P, 4, E], BF16)
        place = sb("place", [P, C, E])
        picked = sb("picked", [P, C, K, E])
        dest = sb("dest", [P, 4, C, K], U32)
        x1_all = sb("x1_all", [P, TILES, D])
        logit_all = sb("logit_all", [P, TILES, E])
        top_all = sb("top_all", [P, TILES, K])

        count = sb("count", [P, E])
        count_i = sb("count_i", [P, E], I32)
        nblk_i = sb("nblk_i", [P, E], I32)
        nblk = sb("nblk", [P, E])
        upto = sb("upto", [P, E])
        zero8 = sb("zero8", [P, E])
        skip_f = sb("skip_f", [P, E])
        tail_i = sb("tail_i", [P, E], I32)
        passed = sb("passed", [P, BLOCKS, E])
        passed_rows = sb("passed_rows", [P, BLOCKS, E])
        blk_e = sb("blk_e", [P, BLOCKS])
        blk_e7 = sb("blk_e7", [P, BLOCKS])
        blk_e_i = sb("blk_e_i", [P, BLOCKS], I32)
        blk_row = sb("blk_row", [P, BLOCKS])
        blk_row_i = sb("blk_row_i", [P, BLOCKS], I32)

        xb = sb("xb", [P, 4, ROW])
        xbT = sb("xbT", [P, 2, P])
        act1 = sb("act1", [P, 2, H])
        gated = sb("gated", [P, 2, H])
        gatedT = sb("gatedT", [P, 2, HC, P])
        yb = sb("yb", [P, 4, D])
        ydest = sb("ydest", [P, 4, 1], U32)

        shifted = sb("shifted", [P, TILES, E])
        expd = sb("expd", [P, TILES, E])
        total = sb("total", [P, TILES])
        score = sb("score", [P, TILES, K])
        yg = sb("yg", [P, 2, GROUP, K, D])
        sum0 = sb("sum0", [P, 2, GROUP, D])
        sum1 = sb("sum1", [P, 2, GROUP, D])
        stats2 = sb("stats2", [P, 2, GROUP, 6])
        mv2 = sb("mv2", [P, 2, GROUP, 2])
        lnv2 = sb("lnv2", [P, 2, GROUP])
        rstd2 = sb("rstd2", [P, 2, GROUP])
        res = sb("res", [P, 2, GROUP, D])

        bank = [ctx.enter_context(nc.psum_tensor(f"bank{i}", [P, 512], F32)) for i in range(8)]
        xT_ps = bank[0][:, 0:N]
        yv_ps = bank[1][:, :]
        s_ps = bank[2][:, :].rearrange("p (c n) -> p c n", c=C)
        pT_ps = [bank[3][:, 0:N], bank[7][:, 0:N]]
        o_ps = bank[4][:, 0:C * D].rearrange("p (c d) -> p c d", c=C)
        x1T_ps = bank[5][:, 0:N]
        logit_ps = bank[6][:, 0:C * E].rearrange("p (c e) -> p c e", c=C)
        rank_ps = bank[6][:, 64:64 + C * E].rearrange("p (c e) -> p c e", c=C)

        w_loaded = sem("w_loaded")
        e_loaded = sem("e_loaded")
        made = sem("made")
        made_v = sem("made_v")
        prep_ps = sem("prep_ps")
        prep_sb = sem("prep_sb")
        x_loaded = sems("x_loaded", 4)
        xT_ready = sem("xT_ready")
        xT_kept = sem("xT_kept")
        yv_ready = sem("yv_ready")
        yv_kept = sem("yv_kept")
        s_ready = sem("s_ready")
        nmax_ready = sem("nmax_ready")
        prob_ready = sem("prob_ready")
        pT_ready = sem("pT_ready")
        pT0_kept = sem("pT0_kept")
        pT1_kept = sem("pT1_kept")
        o_ready = sem("o_ready")
        hid_ready = sem("hid_ready")
        rinv_ready = sem("rinv_ready")
        stats_ready = sem("stats_ready")
        mv_ready = sem("mv_ready")
        lnv_ready = sem("lnv_ready")
        rstd_ready = sem("rstd_ready")
        x1_ready = sem("x1_ready")
        x1T_ready = sem("x1T_ready")
        x1T_kept = sem("x1T_kept")
        logit_ready = sem("logit_ready")
        top_ready = sem("top_ready")
        best_ready = sem("best_ready")
        onehot_ready = sem("onehot_ready")
        chosen_ready = sem("chosen_ready")
        seen_ready = sem("seen_ready")
        rank_ready = sem("rank_ready")
        place_ready = sem("place_ready")
        picked_ready = sem("picked_ready")
        dest_ready = sem("dest_ready")
        tagged = sem("tagged")
        pool_turns = sem("pool_turns")
        scattered = sems("scattered", 4)
        x1_copied = sems("x1_copied", 4)

        count_ready = sem("count_ready")
        table = sem("table")
        padded = sem("padded")
        xb_loaded = sems("xb_loaded", 4)
        xbT_ready = sem("xbT_ready")
        xbT_kept = sem("xbT_kept")
        h_ready = sem("h_ready")
        act_ready = sem("act_ready")
        gated_ready = sem("gated_ready")
        gT_ready = sem("gT_ready")
        gT_kept = sem("gT_kept")
        y_ready = sem("y_ready")
        y_kept = sem("y_kept")
        ydest_ready = sem("ydest_ready")
        y_scattered = sems("y_scattered", 4)

        score_steps = sem("score_steps")
        exp_ready = sem("exp_ready")
        yg_loaded = sems("yg_loaded", 2)
        sum0_ready = sem("sum0_ready")
        sum1_ready = sem("sum1_ready")
        stats2_ready = sem("stats2_ready")
        mv2_ready = sem("mv2_ready")
        lnv2_ready = sem("lnv2_ready")
        rstd2_ready = sem("rstd2_ready")
        res_ready = sem("res_ready")
        stored = sems("stored", 2)

        TABLE_DONE = 12

        WHOLE = (6, 29)
        LAST = BATCHES - 1 + 5
        WHOLE2 = (4, BLOCKS - 5)
        LAST2 = BLOCKS - 1 + 2

        block = ctx.enter_context(nc.Block())

        def store(sp, g):
            sp.wait_ge(res_ready, GROUP * (g + 1))
            sp.dma_start(out_groups[:, g * GROUP:(g + 1) * GROUP, :], res[:, g % 2]).then_inc(stored[g % 2], 16)

        @block.sync
        def _(sp):
            sp.dma_start(w_in[:], w_qkv.rearrange("(j e) d -> e j d", e=P)).then_inc(w_loaded, 16)
            sp.dma_start(gate_in[:], gate_w).then_inc(w_loaded, 16)

            def load(b):
                wait(sp, hid_ready, (b - 3).number)
                sp.dma_start(xin[:, b.slot], x_tiles[b.number]).then_inc(x_loaded[b.slot], 16)

            def keep(b):
                sp.wait_ge(x1_ready, (b + 1).number)
                sp.dma_start(x1_all[:, bass.ds(b.number * C, C), :], x1[:, b.slot, :, 0:D])\
                    .then_inc(x1_copied[b.slot], 16)

            def step(i):
                if (i + 2).valid(BATCHES):
                    load(i + 2)
                if (i - 2).valid(BATCHES):
                    keep(i - 2)

            load(At(0, 0))
            load(At(0, 1))
            for e in range(E):
                sp.dma_start(w13[:, e, 0, :], w1[e]).then_inc(e_loaded, 16)
                sp.dma_start(w13[:, e, 1, :], w3[e]).then_inc(e_loaded, 16)
                sp.dma_start(w2s[:, e], w2[e].rearrange("(c h) d -> h c d", h=P)).then_inc(e_loaded, 16)
            steps(sp, *WHOLE, LAST, step)

            sp.wait_ge(made_v, 9)
            sp.dma_start(rows_dram[DUMMY:DUMMY + P, :], padding[:]).then_inc(padded, 16)
            sp.wait_ge(table, TABLE_DONE)
            for s in range(4):
                sp.wait_ge(scattered[s], BATCHES // 4 * C * K * 16)
            for e in range(E):
                tail = sp.value_load(tail_i[0:1, e:e + 1], min_val=0, max_val=DUMMY - P)
                sp.dma_start(rows_dram[bass.ds(tail, P), :], padding[:]).then_inc(padded, 16)
            sp.wait_ge(padded, 16 * (E + 1))

            def load_block(j):
                row = sp.value_load(blk_row_i[0:1, bass.ds(j.number, 1)], min_val=0, max_val=DUMMY)
                wait(sp, xbT_ready, (j - 3).number)
                wait(sp, ydest_ready, (j - 3).number)
                sp.dma_start(xb[:, j.slot, :], rows_dram[bass.ds(row, P), :])\
                    .then_inc(xb_loaded[j.slot], 16)

            steps(sp, 4, BLOCKS - 1, BLOCKS - 1, load_block)

            for s in range(4):
                sp.wait_ge(y_scattered[s], BLOCKS // 4 * 16)
            for g in range(GROUPS):
                wait(sp, sum1_ready, GROUP * (g - 1))
                sp.dma_start(yg[:, g % 2].rearrange("p t k d -> p t (k d)"),
                             y_groups[:, g * GROUP:(g + 1) * GROUP, :]).then_inc(yg_loaded[g % 2], 16)
                if g >= 1:
                    store(sp, g - 1)
            store(sp, GROUPS - 1)
            for s in range(2):
                sp.wait_ge(stored[s], GROUPS // 2 * 16)

        @block.gpsimd
        def _(pool):
            pool.memset(ident[:], 0.0).then_inc(made, 1)
            pool.memset(before[:], 1.0).then_inc(made, 1)
            pool.memset(ones[:], 1.0).then_inc(made, 1)
            pool.wait_ge(made, 2)
            pool.affine_select(out=ident[:], in_=ident[:], compare_op=ALU.not_equal, fill=1.0,
                               base=0, pattern=[[-1, P]], channel_multiplier=1).then_inc(made, 1)
            pool.affine_select(out=before[:], in_=before[:], compare_op=ALU.is_gt, fill=0.0,
                               base=0, pattern=[[1, P]], channel_multiplier=-1).then_inc(made, 1)
            pool.iota(lane_i[:], [[1, 8]], 0, 0).then_inc(made, 1)
            pool.iota(block_i[:], [[1, BLOCKS]], 0, 0).then_inc(made, 1)
            pool.iota(token_i[:], [[2 * P, TILES]], 0, 2).then_inc(made, 1)

            def scatter(b):
                pool.wait_ge(dest_ready, (b + 1).number)
                pool.wait_ge(tagged, (b + 1).number)
                pool.sem_inc(pool_turns)
                for c in range(C):
                    for k in range(K):
                        pool.indirect_dma_start(
                            out=rows_dram, in_=x1[:, b.slot, c, :], in_offset=None,
                            out_offset=bass.IndirectOffsetOnAxis(ap=dest[:, b.slot, c, k:k + 1], axis=0)).then_inc(scattered[b.slot], 16)

            def step(i):
                if (i - 5).valid(BATCHES):
                    scatter(i - 5)

            steps(pool, *WHOLE, LAST, step)

            last_row = pool.alloc_register("last_row")
            pool.reg_mov(last_row, 2 * TOKENS - 1)

            def scatter_y(j):
                pool.wait_ge(y_kept, (j + 1).number)
                pool.wait_ge(ydest_ready, (j + 1).number)
                pool.sem_inc(pool_turns)
                pool.indirect_dma_start(
                    out=y_dram, in_=yb[:, j.slot, :], in_offset=None,
                    out_offset=bass.IndirectOffsetOnAxis(ap=ydest[:, j.slot, :], axis=0),
                    bounds_check=last_row, oob_is_err=False).then_inc(y_scattered[j.slot], 16)

            def step2(j):
                if (j - 2).valid(BLOCKS):
                    scatter_y(j - 2)

            steps(pool, *WHOLE2, LAST2, step2)

        @block.scalar
        def _(act):
            act.preload_act_table_set("natural_log_exp_and_others")
            act.wait_ge(prep_ps, 1)
            act.activation(wqk[:], bank[0][:, 0:D], ACT.Copy, scale=SCALE).then_inc(prep_sb, 1)
            act.wait_ge(prep_ps, 2)
            act.activation(wvT[:], bank[1][:, 0:D], ACT.Copy).then_inc(prep_sb, 1)
            act.wait_ge(prep_ps, 3)
            act.activation(gateT[:], bank[2][:, 0:E], ACT.Copy).then_inc(prep_sb, 1)

            def keep_xT(b):
                act.wait_ge(xT_ready, (b + 1).number)
                wait(act, s_ready, (b - 1).number)
                act.activation(xT[:, b.half], xT_ps, ACT.Copy).then_inc(xT_kept, 1)

            def keep_yv(b):
                act.wait_ge(yv_ready, (b + 1).number)
                wait(act, o_ready, (b - 1).number)
                act.activation(yv[:, b.half].rearrange("p j n -> p (j n)"), yv_ps, ACT.Copy)\
                    .then_inc(yv_kept, 1)

            def exponent(b):
                act.wait_ge(nmax_ready, (b + 1).number)
                wait(act, pT_ready, (b - 1).number)
                wait(act, rinv_ready, (b - 1).number)
                for c in range(C):
                    ins = act.activation(prob[:, b.half, c, :], s_ps[:, c, :], ACT.Exp,
                                         bias=nmax[:, b.half, c:c + 1],
                                         accum_out=psum_[:, b.half, c:c + 1])
                    ins.then_inc(prob_ready, 1)

            def keep_pT(b):
                act.wait_ge(pT_ready, (b + 1).number)
                wait(act, o_ready, (b - 1).number)
                act.activation(probT[:, b.half, 0, :], pT_ps[0], ACT.Copy).then_inc(pT0_kept, 1)

            def keep_x1T(b):
                act.wait_ge(x1T_ready, (b + 1).number)
                wait(act, logit_ready, (b - 1).number)
                act.activation(x1T[:, b.half], x1T_ps, ACT.Copy).then_inc(x1T_kept, 1)

            def deviation(b):
                act.wait_ge(mv_ready, (b + 1).number * C)
                act.activation(lnv[:], mv[:, b.half, :, 1:2], ACT.Ln, bias=eps_col[:, 0:1]).then_inc(lnv_ready, 1)
                act.wait_ge(lnv_ready, (b + 1).number)
                wait(act, x1_ready, (b - 1).number)
                act.activation(rstd[:, b.half, :], lnv[:, :, 0], ACT.Exp, scale=-0.5).then_inc(rstd_ready, 1)

            def tag(b):
                act.wait_ge(best_ready, (b + 1).number * C)
                act.activation(x1[:, b.slot, :, D + 1], best[:, b.half, :, 0], ACT.Copy)
                act.activation(x1[:, b.slot, :, D], token_f[:, bass.ds(b.number * C, C)], ACT.Copy)\
                    .then_inc(tagged, 1)

            def step(i):
                if (i - 1).valid(BATCHES):
                    exponent(i - 1)
                if i.valid(BATCHES):
                    keep_yv(i)
                if (i + 1).valid(BATCHES):
                    keep_xT(i + 1)
                if (i - 4).valid(BATCHES):
                    tag(i - 4)
                if (i - 3).valid(BATCHES):
                    keep_x1T(i - 3)
                if (i - 1).valid(BATCHES):
                    keep_pT(i - 1)
                if (i - 2).valid(BATCHES):
                    deviation(i - 2)

            act.wait_ge(made_v, 5)
            keep_xT(At(0, 0))
            steps(act, *WHOLE, LAST, step)

            act.wait_ge(score_steps, 1)
            act.activation(expd[:].rearrange("p t e -> p (t e)"), shifted[:].rearrange("p t e -> p (t e)"),
                           ACT.Exp).then_inc(exp_ready, 1)
            act.wait_ge(exp_ready, 1)
            act.wait_ge(score_steps, 2)
            act.activation(top_all[:, :, 1], top_all[:, :, 1], ACT.Exp).then_inc(exp_ready, 1)
            act.preload_act_table(ACT.Silu)

            def keep_xbT(j):
                act.wait_ge(xbT_ready, (j + 1).number)
                wait(act, h_ready, (j - 1).number)
                act.activation(xbT[:, j.half], bank[j.half][:, 0:P], ACT.Copy).then_inc(xbT_kept, 1)

            def silu(j):
                act.wait_ge(h_ready, (j + 1).number)
                wait(act, gated_ready, (j - 1).number)
                act.activation(act1[:, j.half], bank[2 + j.half][:, 0:H], ACT.Silu).then_inc(act_ready, 1)

            def keep_y(j):
                act.wait_ge(y_ready, (j + 1).number)
                wait(act, y_scattered[j.slot], j.turn * 16)
                act.activation(yb[:, j.slot], bank[6 + j.half][:, 0:D], ACT.Copy).then_inc(y_kept, 1)

            def step2(j):
                if j.valid(BLOCKS):
                    silu(j)
                if (j + 1).valid(BLOCKS):
                    keep_xbT(j + 1)
                if (j - 2).valid(BLOCKS):
                    keep_y(j - 2)

            keep_xbT(At(0, 0))
            steps(act, *WHOLE2, LAST2, step2)

            act.preload_act_table_set("natural_log_exp_and_others")
            for g in range(GROUPS):
                act.wait_ge(mv2_ready, GROUP * (g + 1))
                act.activation(lnv2[:, g % 2, :], mv2[:, g % 2, :, 1], ACT.Ln, bias=eps_col[:, 0:1]).then_inc(lnv2_ready, 1)
                act.wait_ge(lnv2_ready, g + 1)
                wait(act, res_ready, GROUP * (g - 1))
                act.activation(rstd2[:, g % 2, :], lnv2[:, g % 2, :], ACT.Exp, scale=-0.5).then_inc(rstd2_ready, 1)

        @block.tensor
        def _(pe):
            pe.wait_ge(w_loaded, 32)
            pe.wait_ge(made, 5)
            pe.matmul(bank[0][:, 0:D], w_in[:, 0, :], w_in[:, 1, :], start=True, stop=True).then_inc(prep_ps, 1)
            pe.transpose(bank[1][:, 0:D], w_in[:, 2, :], ident[:]).then_inc(prep_ps, 1)
            pe.transpose(bank[2][:, 0:E], gate_in[:, :], ident[0:E, 0:E]).then_inc(prep_ps, 1)
            pe.wait_ge(prep_sb, 3)

            def turn_x(b):
                pe.wait_ge(x_loaded[b.slot], 16 * (b.turn + 1))
                wait(pe, xT_kept, b.number)
                for c in range(C):
                    ins = pe.transpose(xT_ps[:, c * P:(c + 1) * P], xin[:, b.slot, c, :], ident[:])
                ins.then_inc(xT_ready, 1)

            def project(b):
                pe.wait_ge(xT_kept, (b + 1).number)
                wait(pe, yv_kept, b.number)
                pe.matmul(yv_ps[:, 0:N], wqk[:], xT[:, b.half, :], start=True, stop=True)
                for c in range(C):
                    ins = pe.matmul(yv_ps[:, N + c * D:N + (c + 1) * D], xT[:, b.half, c * P:(c + 1) * P],
                                    wvT[:], start=True, stop=True)
                ins.then_inc(yv_ready, 1)

            def weigh(b):
                pe.wait_ge(pT0_kept, (b + 1).number)
                pe.wait_ge(pT1_kept, (b + 1).number)
                wait(pe, hid_ready, b.number)
                for c in range(C):
                    for m in range(C):
                        ins = pe.matmul(o_ps[:, c, :], probT[:, b.half, m, c * P:(c + 1) * P],
                                        yv[:, b.half, 1, m * D:(m + 1) * D], start=(m == 0), stop=(m == C - 1))
                ins.then_inc(o_ready, 1)

            def turn_x1(b):
                pe.wait_ge(x1_ready, (b + 1).number)
                wait(pe, x1T_kept, b.number)
                for c in range(C):
                    ins = pe.transpose(x1T_ps[:, c * P:(c + 1) * P], x1[:, b.slot, c, 0:D], ident[:])
                ins.then_inc(x1T_ready, 1)

            def turn_prob(b):
                pe.wait_ge(prob_ready, (b + 1).number * C)
                wait(pe, pT0_kept, b.number)
                wait(pe, pT1_kept, b.number)
                for m in range(C):
                    for c in range(C):
                        ins = pe.transpose(pT_ps[m][:, c * P:(c + 1) * P],
                                           prob[:, b.half, c, m * P:(m + 1) * P], ident[:])
                ins.then_inc(pT_ready, 1)

            def score_(b):
                pe.wait_ge(yv_kept, (b + 1).number)
                wait(pe, prob_ready, b.number * C)
                for c in range(C):
                    ins = pe.matmul(s_ps[:, c, :], yv[:, b.half, 0, c * P:(c + 1) * P], xT[:, b.half, :],
                                    start=True, stop=True)
                ins.then_inc(s_ready, 1)

            def rank(b):
                pe.wait_ge(seen_ready, (b + 1).number * C)
                pe.matmul(rank_ps.rearrange("p c e -> p (c e)"), before[:],
                          chosen[:, b.half].rearrange("p c e -> p (c e)"), start=True, stop=False)
                at = 2 * b.half
                pe.matmul(rank_ps.rearrange("p c e -> p (c e)"), ones[:],
                          seen[:, at:at + C].rearrange("p c e -> p (c e)"), start=False, stop=True)\
                    .then_inc(rank_ready, 1)

            def route(b):
                pe.wait_ge(x1T_kept, (b + 1).number)
                for c in range(C):
                    ins = pe.matmul(logit_ps[:, c, :], x1T[:, b.half, c * P:(c + 1) * P], gateT[:],
                                    start=True, stop=True)
                ins.then_inc(logit_ready, 1)

            def step(i):
                if i.valid(BATCHES):
                    project(i)
                if (i + 1).valid(BATCHES):
                    turn_x(i + 1)
                if (i - 2).valid(BATCHES):
                    weigh(i - 2)
                if (i - 3).valid(BATCHES):
                    turn_x1(i - 3)
                if (i - 1).valid(BATCHES):
                    turn_prob(i - 1)
                if i.valid(BATCHES):
                    score_(i)
                if (i - 4).valid(BATCHES):
                    wait(pe, best_ready, (i - 3).number * C)
                    wait(pe, place_ready, (i - 4).number)
                    rank(i - 4)
                if (i - 3).valid(BATCHES):
                    route(i - 3)

            turn_x(At(0, 0))
            steps(pe, *WHOLE, LAST, step)
            pe.wait_ge(place_ready, BATCHES)
            pe.wait_ge(seen_ready, BATCHES * C)
            pe.matmul(bank[6][:, 0:E], ones[:], seen[:, 0, :], start=True, stop=True).then_inc(count_ready, 1)
            pe.wait_ge(e_loaded, 16 * 3 * E)
            pe.wait_ge(table, TABLE_DONE)

            def turn_block(j):
                pe.wait_ge(xb_loaded[j.slot], 16 * (j.turn + 1))
                wait(pe, xbT_kept, (j - 1).number)
                pe.transpose(bank[j.half][:, 0:P], xb[:, j.slot, 0:D], ident[:]).then_inc(xbT_ready, 1)

            def up(j):
                expert = pe.value_load(blk_e_i[0:1, bass.ds(j.number, 1)], min_val=0, max_val=E - 1)
                pe.wait_ge(xbT_kept, (j + 1).number)
                wait(pe, gated_ready, (j - 1).number)
                pe.matmul(bank[2 + j.half][:, :], xbT[:, j.half, :],
                          w13[:].rearrange("p e j h -> p (e j h)")[:, bass.ds(expert * (2 * H), 2 * H)],
                          start=True, stop=True).then_inc(h_ready, 1)

            def turn_gated(j):
                pe.wait_ge(gated_ready, (j + 1).number)
                wait(pe, gT_kept, (j - 1).number)
                for h in range(HC):
                    ins = pe.transpose(bank[4 + j.half][:, h * P:(h + 1) * P],
                                       gated[:, j.half, h * P:(h + 1) * P], ident[:])
                ins.then_inc(gT_ready, 1)

            def down(j):
                expert = pe.value_load(blk_e_i[0:1, bass.ds(j.number, 1)], min_val=0, max_val=E - 1)
                pe.wait_ge(gT_kept, (j + 1).number)
                wait(pe, y_kept, (j - 1).number)
                for h in range(HC):
                    ins = pe.matmul(bank[6 + j.half][:, 0:D], gatedT[:, j.half, h, :],
                                    w2s[:].rearrange("p e c d -> p (e c d)")[
                                        :, bass.ds(expert * (HC * D) + h * D, D)],
                                    start=(h == 0), stop=(h == HC - 1))
                ins.then_inc(y_ready, 1)

            def step2(j):
                if j.valid(BLOCKS):
                    up(j)
                if (j + 1).valid(BLOCKS):
                    turn_block(j + 1)
                if (j - 1).valid(BLOCKS):
                    turn_gated(j - 1)
                if (j - 2).valid(BLOCKS):
                    down(j - 2)

            turn_block(At(0, 0))
            steps(pe, *WHOLE2, LAST2, step2)

        @block.vector
        def _(ve):
            ve.memset(seen[:], 0.0).then_inc(made_v, 1)
            ve.memset(zero8[:], 0.0).then_inc(made_v, 1)
            ve.memset(eps_col[:], EPS).then_inc(made_v, 1)
            ve.wait_ge(made, 8)
            ve.tensor_copy(token_f[:], token_i[:]).then_inc(made_v, 1)
            ve.memset(padding[:], 0.0).then_inc(made_v, 1)
            ve.wait_ge(made_v, 5)
            ve.memset(padding[:, D:D + 1], float(SKIP)).then_inc(made_v, 1)
            ve.tensor_copy(block_f[:], block_i[:]).then_inc(made_v, 1)
            ve.tensor_copy(lane_f[:], lane_i[:]).then_inc(made_v, 1)
            ve.wait_ge(made_v, 8)
            ve.tensor_scalar(region_f[:], lane_f[:], float(REGION), None, ALU.mult).then_inc(made_v, 1)
            ve.wait_ge(made_v, 9)

            def row_max(b):
                ve.wait_ge(s_ready, (b + 1).number)
                wait(ve, prob_ready, (b - 1).number * C)
                ve.tensor_reduce(nmax[:, b.half, :], s_ps, X, ALU.max, negate=True).then_inc(nmax_ready, 1)

            def choose_a(b):
                ve.wait_ge(logit_ready, (b + 1).number)
                wait(ve, tagged, (b - 1).number)
                ve.tensor_scalar(logit_all[:, bass.ds(b.number * C, C), :], logit_ps, 1.0, None, ALU.mult)
                for c in range(C):
                    ve.max(top[:, b.half, c, :], logit_ps[:, c, :]).then_inc(top_ready, 1)
                ve.wait_ge(top_ready, (b + 1).number * C)
                ve.tensor_scalar(top_all[:, bass.ds(b.number * C, C), :], top[:, b.half, :, 0:K], 1.0, None,
                                 ALU.mult)
                for c in range(C):
                    ve.max_index(best[:, b.half, c, :], top[:, b.half, c, :], logit_ps[:, c, :])\
                        .then_inc(best_ready, 1)

            def choose_b(b):
                ve.wait_ge(best_ready, (b + 1).number * C)
                ve.tensor_tensor(onehot[:, b.half], lane_f[:, None, None, :].broadcast_to([P, C, K, E]),
                                 best[:, b.half, :, 0:K, None].broadcast_to([P, C, K, E]),
                                 ALU.is_equal).then_inc(onehot_ready, 1)

            def choose_c(b):
                ve.wait_ge(onehot_ready, (b + 1).number)
                wait(ve, rank_ready, (b - 1).number)
                ve.tensor_tensor(chosen[:, b.half], onehot[:, b.half, :, 0, :], onehot[:, b.half, :, 1, :],
                                 ALU.add).then_inc(chosen_ready, 1)

            def choose_d(b):
                ve.wait_ge(chosen_ready, (b + 1).number)
                at = 2 * b.half
                ve.tensor_tensor(seen[:, at + 1], seen[:, at], chosen[:, b.half, 0], ALU.add)\
                    .then_inc(seen_ready, 1)
                ve.wait_ge(seen_ready, b.number * C + 1)
                wait(ve, rank_ready, b.number)
                ve.tensor_tensor(seen[:, (at + 2) % 4], seen[:, at + 1], chosen[:, b.half, 1], ALU.add)\
                    .then_inc(seen_ready, 1)

            def place_a(b):
                ve.wait_ge(rank_ready, (b + 1).number)
                if (b + 1).valid(BATCHES):
                    ve.wait_ge(logit_ready, (b + 2).number)
                ve.tensor_tensor(place[:], rank_ps, region_f[:, None, :].broadcast_to([P, C, E]), ALU.add)\
                    .then_inc(place_ready, 1)

            def place_b(b):
                ve.wait_ge(place_ready, (b + 1).number)
                ve.tensor_tensor(picked[:], onehot[:, b.half],
                                 place[:, :, None, :].broadcast_to([P, C, K, E]), ALU.mult)\
                    .then_inc(picked_ready, 1)

            def place_c(b):
                ve.wait_ge(picked_ready, (b + 1).number)
                wait(ve, scattered[b.slot], b.turn * (C * K * 16))
                with nc.allow_low_precision(reason="row numbers, whole and below 2 ** 24"):
                    ve.tensor_reduce(dest[:, b.slot], picked[:], X, ALU.add).then_inc(dest_ready, 1)

            def residual(b):
                ve.wait_ge(prob_ready, (b + 1).number * C)
                ve.reciprocal(rinv[:, b.half], psum_[:, b.half]).then_inc(rinv_ready, 1)
                ve.wait_ge(rinv_ready, (b + 1).number)
                ve.wait_ge(o_ready, (b + 1).number)
                ve.wait_ge(x_loaded[b.slot], 16 * (b.turn + 1))
                for c in range(C):
                    ins = ve.scalar_tensor_tensor(out=hid[:, b.half, c, :], in0=o_ps[:, c, :],
                                                  scalar=rinv[:, b.half, c:c + 1],
                                                  in1=xin[:, b.slot, c, :], op0=ALU.mult, op1=ALU.add)
                ins.then_inc(hid_ready, 1)

            def statistics(b):
                ve.wait_ge(hid_ready, (b + 1).number)
                for c in range(C):
                    ve.bn_stats(stats[:, c, :], hid[:, b.half, c, :]).then_inc(stats_ready, 1)

            def aggregate(b):
                for c in range(C):
                    ve.bn_aggr(mv[:, b.half, c, :], stats[:, c, :]).then_inc(mv_ready, 1)

            def keep_pT(b):
                ve.wait_ge(pT_ready, (b + 1).number)
                wait(ve, o_ready, (b - 1).number)
                ve.tensor_copy(probT[:, b.half, 1, :], pT_ps[1]).then_inc(pT1_kept, 1)

            def normalise(b):
                ve.wait_ge(rstd_ready, (b + 1).number)
                ve.wait_ge(mv_ready, (b + 1).number * C)
                wait(ve, scattered[b.slot], b.turn * (C * K * 16))
                wait(ve, x1_copied[b.slot], b.turn * 16)
                for c in range(C):
                    ins = ve.tensor_scalar(x1[:, b.slot, c, 0:D], hid[:, b.half, c, :],
                                           mv[:, b.half, c, 0:1], rstd[:, b.half, c:c + 1],
                                           ALU.subtract, ALU.mult)
                ins.then_inc(x1_ready, 1)

            def step(i):
                if (i - 1).valid(BATCHES):
                    row_max(i - 1)
                if (i - 5).valid(BATCHES):
                    place_a(i - 5)
                if (i - 4).valid(BATCHES):
                    choose_a(i - 4)
                if (i - 5).valid(BATCHES):
                    place_b(i - 5)
                if (i - 4).valid(BATCHES):
                    choose_b(i - 4)
                if (i - 5).valid(BATCHES):
                    place_c(i - 5)
                if (i - 4).valid(BATCHES):
                    choose_c(i - 4)
                    choose_d(i - 4)
                if (i - 2).valid(BATCHES):
                    residual(i - 2)
                    statistics(i - 2)
                    ve.wait_ge(stats_ready, (i - 1).number * C)
                if (i - 1).valid(BATCHES):
                    keep_pT(i - 1)
                if (i - 2).valid(BATCHES):
                    aggregate(i - 2)
                    normalise(i - 2)

            steps(ve, *WHOLE, LAST, step)

            made_steps = [0]

            def tabled(ins):
                made_steps[0] += 1
                ins.then_inc(table, 1)
                ve.wait_ge(table, made_steps[0])

            ve.wait_ge(count_ready, 1)
            tabled(ve.tensor_copy(count[:], bank[6][:, 0:E]))
            tabled(ve.tensor_tensor(tail_i[:], count[:], region_f[:], ALU.add))
            tabled(ve.tensor_scalar(count_i[:], count[:], float(P - 1), None, ALU.add))
            tabled(ve.tensor_scalar(nblk_i[:], count_i[:], 7, None, ALU.logical_shift_right))
            tabled(ve.tensor_copy(nblk[:], nblk_i[:]))
            tabled(ve.tensor_tensor_scan(upto[:], nblk[:], zero8[:], 0.0, ALU.add, ALU.add))
            tabled(ve.tensor_scalar(skip_f[:], nblk[:], float(-P), float(REGION), ALU.mult, ALU.add))
            tabled(ve.tensor_tensor(passed[:], upto[:, None, :].broadcast_to([P, BLOCKS, E]),
                                    block_f[:, :, None].broadcast_to([P, BLOCKS, E]), ALU.is_le))
            ve.tensor_reduce(blk_e[:], passed[:], X, ALU.add)
            tabled(ve.tensor_tensor(passed_rows[:], passed[:], skip_f[:, None, :].broadcast_to([P, BLOCKS, E]),
                                    ALU.mult))
            tabled(ve.tensor_reduce(blk_row[:], passed_rows[:], X, ALU.add))
            tabled(ve.scalar_tensor_tensor(out=blk_row[:], in0=block_f[:], scalar=float(P), in1=blk_row[:],
                                           op0=ALU.mult, op1=ALU.add))
            ve.tensor_scalar(blk_e_i[:], blk_e[:], float(E - 1), None, ALU.min)
            ve.tensor_scalar(blk_row_i[:], blk_row[:], float(DUMMY), None, ALU.min).then_inc(table, 1)
            made_steps[0] += 1
            assert made_steps[0] == TABLE_DONE
            ve.tensor_tensor(shifted[:], logit_all[:], top_all[:, :, 0:1].broadcast_to([P, TILES, E]),
                             ALU.subtract).then_inc(score_steps, 1)
            ve.wait_ge(score_steps, 1)
            ve.tensor_tensor(top_all[:, :, 1], top_all[:, :, 1], top_all[:, :, 0], ALU.subtract)\
                .then_inc(score_steps, 1)
            ve.wait_ge(table, TABLE_DONE)

            def multiply(j):
                ve.wait_ge(act_ready, (j + 1).number)
                wait(ve, gT_ready, (j - 1).number)
                ve.tensor_tensor(gated[:, j.half], act1[:, j.half], bank[2 + j.half][:, H:2 * H], ALU.mult)\
                    .then_inc(gated_ready, 1)

            def keep_gT(j):
                ve.wait_ge(gT_ready, (j + 1).number)
                wait(ve, y_ready, (j - 1).number)
                ve.tensor_copy(gatedT[:, j.half].rearrange("p c t -> p (c t)"), bank[4 + j.half][:, 0:H])\
                    .then_inc(gT_kept, 1)

            def aim(j):
                ve.wait_ge(xb_loaded[j.slot], 16 * (j.turn + 1))
                wait(ve, y_scattered[j.slot], j.turn * 16)
                ve.scalar_tensor_tensor(out=ydest[:, j.slot, :], in0=xb[:, j.slot, D + 1:D + 2],
                                        scalar=blk_e[:, bass.ds(j.number, 1)], in1=xb[:, j.slot, D:D + 1],
                                        op0=ALU.not_equal, op1=ALU.add).then_inc(ydest_ready, 1)

            def step2(j):
                if (j - 1).valid(BLOCKS):
                    keep_gT(j - 1)
                if j.valid(BLOCKS):
                    aim(j)
                    multiply(j)

            steps(ve, *WHOLE2, LAST2, step2)

            ve.wait_ge(exp_ready, 2)
            ve.tensor_reduce(total[:], expd[:], X, ALU.add).then_inc(score_steps, 1)
            ve.wait_ge(score_steps, 3)
            ve.reciprocal(score[:, :, 0], total[:]).then_inc(score_steps, 1)
            ve.wait_ge(score_steps, 4)
            ve.tensor_tensor(score[:, :, 1], score[:, :, 0], top_all[:, :, 1], ALU.mult).then_inc(score_steps, 1)
            ve.wait_ge(score_steps, 5)
            for s in range(4):
                ve.wait_ge(x1_copied[s], BATCHES // 4 * 16)

            def combine(g):
                h = g % 2
                ve.wait_ge(yg_loaded[h], 16 * (g // 2 + 1))
                for t in range(GROUP):
                    tile = g * GROUP + t
                    ve.scalar_tensor_tensor(out=sum0[:, h, t, :], in0=yg[:, h, t, 0, :],
                                            scalar=score[:, tile, 0:1], in1=x1_all[:, tile, :],
                                            op0=ALU.mult, op1=ALU.add).then_inc(sum0_ready, 1)
                for t in range(GROUP):
                    tile = g * GROUP + t
                    ve.wait_ge(sum0_ready, tile + 1)
                    ve.scalar_tensor_tensor(out=sum1[:, h, t, :], in0=yg[:, h, t, 1, :],
                                            scalar=score[:, tile, 1:2], in1=sum0[:, h, t, :],
                                            op0=ALU.mult, op1=ALU.add).then_inc(sum1_ready, 1)
                for t in range(GROUP):
                    ve.wait_ge(sum1_ready, g * GROUP + t + 1)
                    ve.bn_stats(stats2[:, h, t, :], sum1[:, h, t, :]).then_inc(stats2_ready, 1)
                wait(ve, rstd2_ready, g - 1)
                for t in range(GROUP):
                    ve.wait_ge(stats2_ready, g * GROUP + t + 1)
                    ve.bn_aggr(mv2[:, h, t, :], stats2[:, h, t, :]).then_inc(mv2_ready, 1)

            def finish(g):
                h = g % 2
                ve.wait_ge(rstd2_ready, g + 1)
                wait(ve, stored[h], g // 2 * 16)
                for t in range(GROUP):
                    ve.tensor_scalar(res[:, h, t, :], sum1[:, h, t, :], mv2[:, h, t, 0:1], rstd2[:, h, t:t + 1],
                                     ALU.subtract, ALU.mult).then_inc(res_ready, 1)

            for g in range(GROUPS):
                combine(g)
                if g >= 1:
                    finish(g - 1)
            finish(GROUPS - 1)


_INS = ["L0_attn_x", "L0_attn_W_qkv", "L0_ffn_gate_w", "L0_ffn_w1", "L0_ffn_w2", "L0_ffn_w3"]


def kernel(**inputs):
    import numpy as _np
    import concourse.bacc as _bacc
    from concourse import mybir as _mybir
    from concourse.bass_utils import run_bass_kernel_spmd as _run

    nc = _bacc.Bacc("TRN2", target_bir_lowering=False, num_devices=1)
    arrays, args = {}, []
    for name in _INS:
        a = _np.ascontiguousarray(inputs[name])
        arrays[f"in_{name}_dram"] = a
        args.append(nc.dram_tensor(f"in_{name}_dram", a.shape, _mybir.dt.from_np(a.dtype), kind="ExternalInput").ap())
    shape = inputs["L0_attn_x"].shape
    args.append(nc.dram_tensor("out_0_dram", shape, _mybir.dt.float32, kind="ExternalOutput").ap())
    attention_moe(nc, *args)
    r = _run(nc, [arrays], core_ids=[0])
    return r.results[0]["out_0_dram"]
```

```python
from contextlib import ExitStack

import concourse.bass as bass
from concourse import mybir

F32 = mybir.dt.float32
BF16 = mybir.dt.bfloat16
I32 = mybir.dt.int32
U32 = mybir.dt.uint32
ALU = mybir.AluOpType
ACT = mybir.ActivationFunctionType
X = mybir.AxisListType.X

P = 128
EPS = 1e-5


class At:

    def __init__(self, quarter, offset):
        self.quarter, self.offset = quarter, offset

    def __add__(self, n):
        return At(self.quarter, self.offset + n)

    def __sub__(self, n):
        return At(self.quarter, self.offset - n)

    @property
    def number(self):
        return self.quarter * 4 + self.offset

    @property
    def slot(self):
        return self.offset % 4

    @property
    def half(self):
        return self.offset % 2

    @property
    def turn(self):
        return self.quarter + self.offset // 4

    def valid(self, count):
        return not isinstance(self.quarter, int) or 0 <= self.number < count


def wait(engine, semaphore, value):
    if not isinstance(value, int) or value > 0:
        engine.wait_ge(semaphore, value)


def steps(engine, first_whole, last_whole, last, step):
    turns = (last_whole + 1 - first_whole) // 4
    for n in range(first_whole):
        step(At(0, n))
    with engine.Fori(0, turns) as turn:
        for n in range(4):
            step(At(turn, first_whole + n))
    for n in range(first_whole + 4 * turns, last + 1):
        step(At(0, n))


def pair_path(experts):
    path, start = [], 1
    for a in range(experts - 1):
        rest = [b for b in range(a + 1, experts) if b != start]
        path += [(a, b) for b in [start] + rest]
        start = path[-1][1] if path[-1][1] > a + 1 else experts - 1
    assert len(set(path)) == experts * (experts - 1) // 2
    assert all(set(p) & set(q) for p, q in zip(path, path[1:]))
    return path


def attention_moe(nc, x, w_qkv, gate_w, w1, w2, w3, out):
    BATCHES, N, D = x.shape
    E, _, H = w1.shape
    C = N // P
    TILES = BATCHES * C
    TOKENS = BATCHES * N
    K = 2
    HC = H // P
    PATH = pair_path(E)
    PAIRS = len(PATH)
    ROW = D + E + 1
    TAG = D + E
    BLOCKS = TOKENS // P
    ITEMS = (K * BLOCKS + PAIRS - 1 + 1) // 2 * 2
    DONE_LAG = PAIRS // 2 + 1
    GROUP = 8
    SCALE = float(D) ** -0.5
    WE = 2 * H
    assert D == P and N == 2 * P and H == 2 * P and BATCHES % 4 == 0 and BLOCKS % 4 == 0 and BLOCKS <= P
    assert K * BLOCKS + PAIRS - 1 <= ITEMS and TILES % GROUP == 0
    assert 2 * DONE_LAG >= K + PAIRS - 1

    x_tiles = x.rearrange("b (c p) d -> b p c d", p=P)
    out_rows = out.rearrange("b n d -> (b n) d")
    rows_dram = nc.dram_tensor("rows", [TOKENS, ROW], F32, kind="Internal").ap()
    row_tiles = rows_dram.rearrange("(b c p) r -> b p c r", p=P, c=C)

    with ExitStack() as ctx:
        def sb(name, shape, dt=F32):
            return ctx.enter_context(nc.sbuf_tensor(name, shape, dt))

        def sem(name):
            return ctx.enter_context(nc.semaphore(name))

        def sems(name, n):
            return [sem(f"{name}{i}") for i in range(n)]

        ident = sb("ident", [P, P])
        before = sb("before", [P, P], BF16)
        ones = sb("ones", [P, P], BF16)
        lane_i = sb("lane_i", [P, E], I32)
        lane_f = sb("lane_f", [P, E])
        one_i = sb("one_i", [P, E], I32)
        bit_i = sb("bit_i", [P, E], I32)
        bit_f = sb("bit_f", [P, E])
        code_i = sb("code_i", [P, PAIRS], I32)
        code_f = sb("code_f", [P, PAIRS])
        has_i = sb("has_i", [P, E, PAIRS], I32)
        has_f = sb("has_f", [P, E, PAIRS])
        item_i = sb("item_i", [P, ITEMS], I32)
        item_f = sb("item_f", [P, ITEMS])
        slot_i = sb("slot_i", [P, BLOCKS], I32)
        slot_f = sb("slot_f", [P, BLOCKS])
        edge_i = sb("edge_i", [P, 1], I32)
        edge_f = sb("edge_f", [P, 2])
        eps_col = sb("eps_col", [P, C])
        minus_half = sb("minus_half", [P, C])
        var = sb("var", [P, C])
        zeros = sb("zeros", [P, PAIRS])
        w_in = sb("w_in", [P, 3, D])
        wqk = sb("wqk", [P, D])
        wvT = sb("wvT", [P, D])
        gate_in = sb("gate_in", [E, D])
        gateT = sb("gateT", [P, E])
        w13 = sb("w13", [P, E, 2, H])
        w2s = sb("w2s", [P, E, WE])

        xin = sb("xin", [P, 4, C, D])
        xT = sb("xT", [P, 2, N])
        yv = sb("yv", [P, 2, 2, N])
        nmax = sb("nmax", [P, 2, C])
        prob = sb("prob", [P, 2, C, N])
        psum_ = sb("psum_", [P, 2, C])
        rinv = sb("rinv", [P, 2, C])
        probT = sb("probT", [P, 2, C, N])
        hid = sb("hid", [P, 2, C, D])
        stats = sb("stats", [P, C, 6])
        mv = sb("mv", [P, 2, C, 2])
        rstd = sb("rstd", [P, 2, C])
        x1 = sb("x1", [P, 4, C, ROW])
        x1T = sb("x1T", [P, 2, N])
        top = sb("top", [P, 2, C, 8])
        best = sb("best", [P, 2, C, 8], U32)
        shifted = sb("shifted", [P, 2, C, E])
        onehot = sb("onehot", [P, 4, C, K, E])
        bits = sb("bits", [P, C, K, E])
        code = sb("code", [P, C])
        pairhot = sb("pairhot", [P, 4, C, PAIRS], BF16)
        seen = sb("seen", [P, 4, PAIRS], BF16)
        picked = sb("picked", [P, C, PAIRS])
        pairhot_all = sb("pairhot_all", [P, TILES, PAIRS], BF16)
        rank_all = sb("rank_all", [P, TILES])
        expd = sb("expd", [P, 4, C, E])
        total = sb("total", [P, 4, C])
        rtotal = sb("rtotal", [P, 4, C])
        chosen = sb("chosen", [P, C, E])
        weight = sb("weight", [P, C, E])

        count = sb("count", [P, PAIRS])
        upto = sb("upto", [P, PAIRS])
        start = sb("start", [P, PAIRS])
        started = sb("started", [P, TILES, PAIRS])
        pos_f = sb("pos_f", [P, TILES])
        pos_i = sb("pos_i", [P, TILES], I32)
        posrow_i = sb("posrow_i", [P, TILES], I32)
        posrow = sb("posrow", [P, TILES])
        posblk_i = sb("posblk_i", [P, TILES], I32)
        posblk = sb("posblk", [P, TILES])
        rowhot = sb("rowhot", [P, 2, GROUP, P])
        blktok = sb("blktok", [P, 2, GROUP, BLOCKS])
        sorted_f = sb("sorted_f", [P, BLOCKS])
        below = sb("below", [BLOCKS, PAIRS])
        inside = sb("inside", [BLOCKS, PAIRS])
        among = sb("among", [BLOCKS, E, PAIRS])
        active = sb("active", [BLOCKS, E])
        scan = sb("scan", [BLOCKS, E], BF16)
        cells = sb("cells", [BLOCKS, E])
        past = sb("past", [BLOCKS, ITEMS, E])
        npast = sb("npast", [BLOCKS, ITEMS], BF16)
        cell_i = sb("cell_i", [1, ITEMS], I32)
        blk_i = sb("blk_i", [1, ITEMS], I32)
        exp_i = sb("exp_i", [1, ITEMS], I32)
        pe_tab = sb("pe_tab", [1, ITEMS + 2, 2], I32)
        ve_tab = sb("ve_tab", [1, ITEMS + 2, 2], I32)
        act_tab = sb("act_tab", [1, ITEMS], I32)

        rows_all = sb("rows_all", [P, BLOCKS + 1, ROW])
        xT_all = sb("xT_all", [P, BLOCKS + 1, P])
        row_in = sb("row_in", [P, 4, ROW])
        w_now = sb("w_now", [P, 2, WE])
        act1 = sb("act1", [P, 2, HC * P])
        gated = sb("gated", [P, 4, HC * P])
        stats2 = sb("stats2", [P, 2, 6])
        mv2 = sb("mv2", [P, 4, 2])
        rstd2 = sb("rstd2", [P, 4, 1])
        res = sb("res", [P, 4, D])
        token = sb("token", [P, 4, 1], U32)
        aim_at = sb("aim_at", [P, 4, 1], U32)
        rows_flat = rows_all[:].rearrange("p b r -> p (b r)")
        xT_flat = xT_all[:].rearrange("p b t -> p (b t)")
        w13_flat = w13[:].rearrange("p e j h -> p (e j h)")
        w2_flat = w2s[:].rearrange("p e c -> p (e c)")

        bank = [ctx.enter_context(nc.psum_tensor(f"bank{i}", [P, 512], F32)) for i in range(8)]
        xT_ps = bank[0][:, 0:N]
        yv_ps = bank[1][:, :]
        s_ps = bank[2][:, :].rearrange("p (c n) -> p c n", c=C)
        pT_ps = [bank[3][:, 0:N], bank[7][:, 0:N]]
        o_ps = bank[4][:, 0:C * D].rearrange("p (c d) -> p c d", c=C)
        x1T_ps = bank[5][:, 0:N]
        logit_ps = bank[6][:, 0:C * E].rearrange("p (c e) -> p c e", c=C)
        rank_ps = bank[6][:, 64:64 + C * PAIRS].rearrange("p (c e) -> p c e", c=C)
        h_ps = [bank[0], bank[1]]
        y_ps = [bank[2], bank[3], bank[4], bank[5]]
        blkT_ps = [bank[6], bank[7]]

        w_loaded = sem("w_loaded")
        e_loaded = sem("e_loaded")
        made = sem("made")
        made_v = sem("made_v")
        prep_ps = sem("prep_ps")
        prep_sb = sem("prep_sb")
        x_loaded = sems("x_loaded", 4)
        xT_ready = sem("xT_ready")
        xT_kept = sem("xT_kept")
        yv_ready = sem("yv_ready")
        yv_kept = sem("yv_kept")
        s_ready = sem("s_ready")
        nmax_ready = sem("nmax_ready")
        prob_ready = sem("prob_ready")
        pT_ready = sem("pT_ready")
        pT0_kept = sem("pT0_kept")
        pT1_kept = sem("pT1_kept")
        o_ready = sem("o_ready")
        hid_ready = sem("hid_ready")
        rinv_ready = sem("rinv_ready")
        stats_ready = sem("stats_ready")
        mv_ready = sem("mv_ready")
        var_ready = sem("var_ready")
        var2_ready = sem("var2_ready")
        rstd_ready = sem("rstd_ready")
        x1_ready = sem("x1_ready")
        x1T_ready = sem("x1T_ready")
        x1T_kept = sem("x1T_kept")
        logit_ready = sem("logit_ready")
        top_ready = sem("top_ready")
        best_ready = sem("best_ready")
        shifted_ready = sem("shifted_ready")
        onehot_ready = sem("onehot_ready")
        bits_ready = sem("bits_ready")
        code_ready = sem("code_ready")
        pairhot_ready = sem("pairhot_ready")
        seen_ready = sem("seen_ready")
        rank_ready = sem("rank_ready")
        picked_ready = sem("picked_ready")
        ranked = sem("ranked")
        expd_ready = sem("expd_ready")
        rtotal_ready = sem("rtotal_ready")
        chosen_ready = sem("chosen_ready")
        weight_ready = sem("weight_ready")
        scored = sem("scored")
        pairs_kept = sem("pairs_kept")
        rows_stored = sems("rows_stored", 4)
        pool_turns = sem("pool_turns")

        count_ready = sem("count_ready")
        table = sem("table")
        pos_ready = sem("pos_ready")
        rowhot_ready = sem("rowhot_ready")
        blktok_ready = sem("blktok_ready")
        group_done = sem("group_done")
        scan_ready = sem("scan_ready")
        blocks_before = sem("blocks_before")
        npast_ready = sem("npast_ready")
        cells_ready = sem("cells_ready")
        aimed = sem("aimed")
        items_known = sem("items_known")
        gathered = sems("gathered", 4)
        turned = sem("turned")
        blkT_kept = sem("blkT_kept")
        w_placed = sem("w_placed")
        h_ready = sem("h_ready")
        act_ready = sem("act_ready")
        gated_ready = sem("gated_ready")
        y_ready = sem("y_ready")
        summed = sem("summed")
        stats2_ready = sem("stats2_ready")
        mv2_ready = sem("mv2_ready")
        rstd2_ready = sem("rstd2_ready")
        res_ready = sem("res_ready")
        stored = sems("stored", 4)

        POOL_CONSTANTS = 11 + PAIRS

        WHOLE = (6, 29)
        LAST = BATCHES - 1 + 5
        STEPS = ITEMS // 2
        WHOLE2 = (DONE_LAG + 2, BLOCKS - 5)
        LAST2 = BLOCKS - 1 + DONE_LAG + 2

        def load_values(engine, registers, table, tops):
            engine.load(registers, table)
            return [nc.s_assert_within(engine.snap(r), 0, top, skip_runtime_bounds_check_because=
                                       "an item's expert is below E, its block at most BLOCKS")
                    for r, top in zip(registers, tops)]

        TOP_EXPERT = (E - 1) * WE
        TOP_BLOCK = BLOCKS * P
        TOP_COLUMN = BLOCKS * ROW

        block = ctx.enter_context(nc.Block())

        @block.sync
        def _(sp):
            sp.dma_start(w_in[:], w_qkv.rearrange("(j e) d -> e j d", e=P)).then_inc(w_loaded, 16)
            sp.dma_start(gate_in[:], gate_w).then_inc(w_loaded, 16)

            def load(b):
                wait(sp, hid_ready, (b - 3).number)
                sp.dma_start(xin[:, b.slot], x_tiles[b.number]).then_inc(x_loaded[b.slot], 16)

            def keep(b):
                sp.wait_ge(scored, (b + 1).number)
                sp.dma_start(row_tiles[b.number], x1[:, b.slot]).then_inc(rows_stored[b.slot], 16)

            def step(i):
                if (i + 2).valid(BATCHES):
                    load(i + 2)
                if (i - 5).valid(BATCHES):
                    keep(i - 5)
                if isinstance(i.quarter, int) and i.number == 2:
                    sp.dma_start(w13[:, :, 0, :], w1.rearrange("e d h -> d e h")).then_inc(e_loaded, 16)
                if isinstance(i.quarter, int) and i.number == 4:
                    sp.dma_start(w13[:, :, 1, :], w3.rearrange("e d h -> d e h")).then_inc(e_loaded, 16)
                if isinstance(i.quarter, int) and i.number == 5:
                    for c in range(HC):
                        sp.dma_start(w2s[:, :, c * D:(c + 1) * D],
                                     w2.rearrange("e (c h) d -> c h e d", h=P)[c]).then_inc(e_loaded, 16)

            load(At(0, 0))
            load(At(0, 1))
            steps(sp, *WHOLE, LAST, step)

        @block.gpsimd
        def _(pool):
            pool.memset(ident[:], 0.0).then_inc(made, 1)
            pool.wait_ge(made, 1)
            pool.affine_select(out=ident[:], in_=ident[:], compare_op=ALU.not_equal, fill=1.0,
                               base=0, pattern=[[-1, P]], channel_multiplier=1).then_inc(made, 1)
            pool.memset(before[:], 1.0).then_inc(made, 1)
            pool.memset(ones[:], 1.0).then_inc(made, 1)
            pool.wait_ge(made, 3)
            pool.affine_select(out=before[:], in_=before[:], compare_op=ALU.is_gt, fill=0.0,
                               base=0, pattern=[[1, P]], channel_multiplier=-1).then_inc(made, 1)
            pool.iota(lane_i[:], [[1, E]], 0, 0).then_inc(made, 1)
            pool.iota(item_i[:], [[1, ITEMS]], 0, 0).then_inc(made, 1)
            pool.iota(slot_i[:], [[P, BLOCKS]], 0, 1).then_inc(made, 1)
            pool.iota(edge_i[:], [[0, 1]], 0, P).then_inc(made, 1)
            pool.memset(eps_col[:], EPS).then_inc(made, 1)
            pool.memset(minus_half[:], -0.5).then_inc(made, 1)
            for q, (a, b) in enumerate(PATH):
                pool.memset(code_i[:, q:q + 1], (1 << a) + (1 << b)).then_inc(made, 1)

            def deviation(b):
                pool.wait_ge(mv_ready, (b + 1).number * C)
                pool.tensor_tensor(var[:, 0:C], mv[:, b.half, :, 1], eps_col[:, 0:C], ALU.add).then_inc(var_ready, 1)
                pool.wait_ge(var_ready, (b + 1).number)
                pool.tensor_tensor(rstd[:, b.half, :], var[:, 0:C], minus_half[:, 0:C], ALU.pow)\
                    .then_inc(rstd_ready, 1)

            def score_rows(b):
                pool.wait_ge(rtotal_ready, (b + 1).number)
                pool.tensor_tensor(chosen[:], onehot[:, b.slot, :, 0, :], onehot[:, b.slot, :, 1, :], ALU.add)\
                    .then_inc(chosen_ready, 1)
                pool.wait_ge(chosen_ready, (b + 1).number)
                pool.tensor_tensor(weight[:], chosen[:], expd[:, b.slot], ALU.mult).then_inc(weight_ready, 1)
                pool.wait_ge(weight_ready, (b + 1).number)
                pool.tensor_tensor(x1[:, b.slot, :, D:D + E], weight[:],
                                   rtotal[:, b.slot, :, None].broadcast_to([P, C, E]), ALU.mult)\
                    .then_inc(scored, 1)

            def keep_pairs(b):
                pool.tensor_tensor(pairhot_all[:, bass.ds(b.number * C, C), :], pairhot[:, b.slot],
                                   pairhot[:, b.slot], ALU.mult).then_inc(pairs_kept, 1)

            def step(i):
                if (i - 5).valid(BATCHES):
                    score_rows(i - 5)
                    keep_pairs(i - 5)
                if (i - 2).valid(BATCHES):
                    deviation(i - 2)

            pool.wait_ge(made, POOL_CONSTANTS)
            steps(pool, *WHOLE, LAST, step)

            pool.wait_ge(pos_ready, 1)
            for g in range(TILES // GROUP):
                wait(pool, group_done, g - 1)
                for t in range(GROUP):
                    tile = g * GROUP + t
                    ins = pool.tensor_scalar(blktok[:, g % 2, t, :], item_f[:, 0:BLOCKS], posblk[:, tile:tile + 1],
                                             slot_f[:, tile:tile + 1], ALU.is_equal, ALU.mult)
                ins.then_inc(blktok_ready, 1)
            for s in range(4):
                pool.wait_ge(rows_stored[s], BATCHES // 4 * 16)

            def gather(n):
                pool.wait_ge(aimed, (n + 1).number)
                pool.sem_inc(pool_turns)
                pool.indirect_dma_start(
                    out=row_in[:, n.slot, :], out_offset=None, in_=rows_dram,
                    in_offset=bass.IndirectOffsetOnAxis(ap=aim_at[:, n.slot, :], axis=0))\
                    .then_inc(gathered[n.slot], 16)

            def deviation2(f):
                pool.wait_ge(mv2_ready, (f + 1).number)
                pool.tensor_tensor(var[:, 0:1], mv2[:, f.slot, 1:2], eps_col[:, 0:1], ALU.add).then_inc(var2_ready, 1)
                pool.wait_ge(var2_ready, (f + 1).number)
                pool.tensor_tensor(rstd2[:, f.slot, :], var[:, 0:1], minus_half[:, 0:1], ALU.pow)\
                    .then_inc(rstd2_ready, 1)

            def scatter_out(f):
                pool.wait_ge(res_ready, (f + 1).number)
                pool.sem_inc(pool_turns)
                pool.indirect_dma_start(
                    out=out_rows, in_=res[:, f.slot, :], in_offset=None,
                    out_offset=bass.IndirectOffsetOnAxis(ap=token[:, f.slot, :], axis=0))\
                    .then_inc(stored[f.slot], 16)

            def step2(m):
                if (m + 4).valid(BLOCKS):
                    gather(m + 4)
                if (m - DONE_LAG - 2).valid(BLOCKS):
                    scatter_out(m - DONE_LAG - 2)
                if (m - DONE_LAG).valid(BLOCKS):
                    deviation2(m - DONE_LAG)

            for n in range(4):
                gather(At(0, n))
            steps(pool, *WHOLE2, LAST2, step2)
            for s in range(4):
                pool.wait_ge(stored[s], BLOCKS // 4 * 16)

        @block.scalar
        def _(act):
            act.preload_act_table(ACT.Exp)
            act.wait_ge(prep_ps, 1)
            act.activation(wqk[:], bank[0][:, 0:D], ACT.Copy, scale=SCALE).then_inc(prep_sb, 1)
            act.wait_ge(prep_ps, 2)
            act.activation(wvT[:], bank[1][:, 0:D], ACT.Copy).then_inc(prep_sb, 1)
            act.wait_ge(prep_ps, 3)
            act.activation(gateT[:], bank[2][:, 0:E], ACT.Copy).then_inc(prep_sb, 1)
            act.wait_ge(made_v, 3)

            def keep_xT(b):
                act.wait_ge(xT_ready, (b + 1).number)
                act.activation(xT[:, b.half], xT_ps, ACT.Copy).then_inc(xT_kept, 1)

            def keep_yv(b):
                act.wait_ge(yv_ready, (b + 1).number)
                act.activation(yv[:, b.half].rearrange("p j n -> p (j n)"), yv_ps, ACT.Copy)\
                    .then_inc(yv_kept, 1)

            def exponent(b):
                act.wait_ge(nmax_ready, (b + 1).number)
                for c in range(C):
                    act.activation(prob[:, b.half, c, :], s_ps[:, c, :], ACT.Exp,
                                   bias=nmax[:, b.half, c:c + 1],
                                   accum_out=psum_[:, b.half, c:c + 1]).then_inc(prob_ready, 1)

            def keep_pT(b):
                act.wait_ge(pT_ready, (b + 1).number)
                act.activation(probT[:, b.half, 0, :], pT_ps[0], ACT.Copy).then_inc(pT0_kept, 1)

            def keep_x1T(b):
                act.wait_ge(x1T_ready, (b + 1).number)
                act.activation(x1T[:, b.half], x1T_ps, ACT.Copy).then_inc(x1T_kept, 1)
                act.activation(x1[:, b.slot, :, TAG], slot_f[:, bass.ds(b.number * C, C)], ACT.Copy)

            def exponent_logits(b):
                act.wait_ge(shifted_ready, (b + 1).number)
                for c in range(C):
                    act.activation(expd[:, b.slot, c, :], shifted[:, b.half, c, :], ACT.Exp,
                                   accum_out=total[:, b.slot, c:c + 1]).then_inc(expd_ready, 1)

            def step(i):
                if (i - 5).valid(BATCHES):
                    exponent_logits(i - 5)
                if (i - 1).valid(BATCHES):
                    exponent(i - 1)
                if i.valid(BATCHES):
                    keep_yv(i)
                if (i - 3).valid(BATCHES):
                    keep_x1T(i - 3)
                if (i - 1).valid(BATCHES):
                    keep_pT(i - 1)
                if (i + 1).valid(BATCHES):
                    keep_xT(i + 1)

            keep_xT(At(0, 0))
            steps(act, *WHOLE, LAST, step)

            act.preload_act_table(ACT.Silu)

            def keep_block(n):
                act.activation(xT_all[:, bass.ds(n.number, 1), :], blkT_ps[n.half][:, None, 0:P], ACT.Copy)\
                    .then_inc(blkT_kept, 1)
                act.activation(rows_all[:, bass.ds(n.number, 1), :], row_in[:, n.slot, None, :], ACT.Copy)

            def silu(m, k):
                act.wait_ge(h_ready, (m.number * 2) + (k + 1))
                act.activation(act1[:, k], h_ps[k][:, 0:HC * P], ACT.Silu).then_inc(act_ready, 1)

            def place_w(k, expert):
                act.activation(w_now[:, k], w13_flat[:, bass.ds(expert, WE)], ACT.Copy).then_inc(w_placed, 1)

            experts = [act.alloc_register(f"expert{k}") for k in range(2)]

            def step2(m):
                if (m + 1).valid(STEPS):
                    expert = load_values(act, experts, act_tab[0:1, bass.ds((m + 1).number * 2, 2)],
                                         [TOP_EXPERT] * 2)
                for k in range(2):
                    if m.valid(STEPS):
                        silu(m, k)
                    if (m + 1).valid(STEPS):
                        place_w(k, expert[k])
                if (m + 2).valid(BLOCKS):
                    keep_block(m + 2)

            for n in range(2):
                act.wait_ge(turned, n + 1)
                keep_block(At(0, n))
            act.wait_ge(e_loaded, 16 * (2 + HC))
            act.wait_ge(items_known, 1)
            expert = load_values(act, experts, act_tab[0:1, 0:2], [TOP_EXPERT] * 2)
            for k in range(2):
                place_w(k, expert[k])
            steps(act, *WHOLE2, LAST2, step2)

        @block.tensor
        def _(pe):
            pe.wait_ge(w_loaded, 32)
            pe.wait_ge(made, 2)
            pe.matmul(bank[0][:, 0:D], w_in[:, 0, :], w_in[:, 1, :], start=True, stop=True).then_inc(prep_ps, 1)
            pe.transpose(bank[1][:, 0:D], w_in[:, 2, :], ident[:]).then_inc(prep_ps, 1)
            pe.transpose(bank[2][:, 0:E], gate_in[:, :], ident[0:E, 0:E]).then_inc(prep_ps, 1)
            pe.wait_ge(prep_sb, 3)
            pe.wait_ge(made, 5)
            pe.wait_ge(made_v, 1)

            def turn_x(b):
                pe.wait_ge(x_loaded[b.slot], 16 * (b.turn + 1))
                for c in range(C):
                    ins = pe.transpose(xT_ps[:, c * P:(c + 1) * P], xin[:, b.slot, c, :], ident[:])
                ins.then_inc(xT_ready, 1)

            def project(b):
                pe.wait_ge(xT_kept, (b + 1).number)
                pe.matmul(yv_ps[:, 0:N], wqk[:], xT[:, b.half, :], start=True, stop=True)
                for c in range(C):
                    ins = pe.matmul(yv_ps[:, N + c * D:N + (c + 1) * D], xT[:, b.half, c * P:(c + 1) * P],
                                    wvT[:], start=True, stop=True)
                ins.then_inc(yv_ready, 1)

            def weigh(b):
                pe.wait_ge(pT0_kept, (b + 1).number)
                pe.wait_ge(pT1_kept, (b + 1).number)
                wait(pe, hid_ready, b.number)
                for c in range(C):
                    for m in range(C):
                        ins = pe.matmul(o_ps[:, c, :], probT[:, b.half, m, c * P:(c + 1) * P],
                                        yv[:, b.half, 1, m * D:(m + 1) * D], start=(m == 0), stop=(m == C - 1))
                ins.then_inc(o_ready, 1)

            def turn_x1(b):
                pe.wait_ge(x1_ready, (b + 1).number)
                for c in range(C):
                    ins = pe.transpose(x1T_ps[:, c * P:(c + 1) * P], x1[:, b.slot, c, 0:D], ident[:])
                ins.then_inc(x1T_ready, 1)

            def turn_prob(b):
                pe.wait_ge(prob_ready, (b + 1).number * C)
                for m in range(C):
                    for c in range(C):
                        ins = pe.transpose(pT_ps[m][:, c * P:(c + 1) * P],
                                           prob[:, b.half, c, m * P:(m + 1) * P], ident[:])
                ins.then_inc(pT_ready, 1)

            def score_(b):
                pe.wait_ge(yv_kept, (b + 1).number)
                for c in range(C):
                    ins = pe.matmul(s_ps[:, c, :], yv[:, b.half, 0, c * P:(c + 1) * P], xT[:, b.half, :],
                                    start=True, stop=True)
                ins.then_inc(s_ready, 1)

            def rank(b):
                pe.wait_ge(seen_ready, (b + 1).number * C)
                pe.matmul(rank_ps.rearrange("p c e -> p (c e)"), before[:],
                          pairhot[:, b.slot].rearrange("p c e -> p (c e)"), start=True, stop=False)
                at = 2 * b.half
                pe.matmul(rank_ps.rearrange("p c e -> p (c e)"), ones[:],
                          seen[:, at:at + C].rearrange("p c e -> p (c e)"), start=False, stop=True)\
                    .then_inc(rank_ready, 1)

            def route(b):
                pe.wait_ge(x1T_kept, (b + 1).number)
                for c in range(C):
                    ins = pe.matmul(logit_ps[:, c, :], x1T[:, b.half, c * P:(c + 1) * P], gateT[:],
                                    start=True, stop=True)
                ins.then_inc(logit_ready, 1)

            def step(i):
                if (i - 2).valid(BATCHES):
                    weigh(i - 2)
                if i.valid(BATCHES):
                    project(i)
                if (i - 3).valid(BATCHES):
                    turn_x1(i - 3)
                if (i - 1).valid(BATCHES):
                    turn_prob(i - 1)
                if i.valid(BATCHES):
                    score_(i)
                if (i + 1).valid(BATCHES):
                    turn_x(i + 1)
                if (i - 4).valid(BATCHES):
                    rank(i - 4)
                if (i - 3).valid(BATCHES):
                    route(i - 3)

            turn_x(At(0, 0))
            steps(pe, *WHOLE, LAST, step)
            pe.wait_ge(picked_ready, BATCHES)
            pe.matmul(bank[6][:, 0:PAIRS], ones[:], seen[:, 0, :], start=True, stop=True).then_inc(count_ready, 1)
            for g in range(TILES // GROUP):
                pe.wait_ge(rowhot_ready, g + 1)
                pe.wait_ge(blktok_ready, g + 1)
                for t in range(GROUP):
                    tile = g * GROUP + t
                    ins = pe.matmul(bank[2][:, 0:BLOCKS], rowhot[:, g % 2, t, :], blktok[:, g % 2, t, :],
                                    start=(tile == 0), stop=(tile == TILES - 1))
                ins.then_inc(group_done, 1)
            pe.wait_ge(scan_ready, 1)
            pe.matmul(bank[0][0:BLOCKS, 0:1], before[0:BLOCKS, 0:BLOCKS], scan[:, E - 1:E],
                      start=True, stop=True).then_inc(blocks_before, 1)
            pe.wait_ge(npast_ready, 1)
            pe.matmul(bank[1][0:1, 0:ITEMS], ones[0:BLOCKS, 0:1], npast[:], start=True, stop=True)\
                .then_inc(cells_ready, 1)

            def turn_block(n):
                pe.wait_ge(gathered[n.slot], 16 * (n.turn + 1))
                pe.transpose(blkT_ps[n.half][:, 0:P], row_in[:, n.slot, 0:D], ident[:]).then_inc(turned, 1)

            def up(m, k, column):
                wait(pe, gated_ready, m.number * 2 + (k - 1))
                pe.wait_ge(w_placed, m.number * 2 + (k + 1))
                for c in range(2 * HC):
                    ins = pe.matmul(h_ps[k][:, c * P:(c + 1) * P],
                                    w_now[:, k, c * P:(c + 1) * P],
                                    xT_flat[:, bass.ds(column, P)], start=True, stop=True)
                ins.then_inc(h_ready, 1)

            def down(m, k, expert):
                at = 2 * m.half + k
                for c in range(HC):
                    ins = pe.matmul(y_ps[at][:, 0:D], gated[:, at, c * P:(c + 1) * P],
                                    w2_flat[:, c * D:][:, bass.ds(expert, D)], start=(c == 0), stop=(c == HC - 1))
                ins.then_inc(y_ready, 1)

            items = [pe.alloc_register(f"item{k}_{what}") for k in range(2) for what in ("expert", "column")]

            def step2(m):
                if m.valid(STEPS + 1):
                    value = load_values(pe, items, pe_tab[:].rearrange("o i j -> o (i j)")[
                        0:1, bass.ds(m.number * 4, 4)], [TOP_EXPERT, TOP_BLOCK] * 2)
                if m.valid(STEPS):
                    pe.wait_ge(blkT_kept, (m + 1).number if (m + 1).valid(BLOCKS + 1) else BLOCKS)
                if (m + 2).valid(BLOCKS):
                    turn_block(m + 2)
                for k in range(2):
                    if m.valid(STEPS):
                        up(m, k, value[2 * k + 1])
                    if (m - 1).valid(STEPS):
                        if not m.valid(STEPS):
                            pe.wait_ge(gated_ready, ITEMS - 1 + k)
                        down(m - 1, k, value[2 * k])

            turn_block(At(0, 0))
            turn_block(At(0, 1))
            pe.wait_ge(items_known, 2)
            steps(pe, *WHOLE2, LAST2, step2)

        @block.vector
        def _(ve):
            ve.memset(seen[:], 0.0).then_inc(made_v, 1)
            ve.memset(zeros[:], 0.0)
            ve.memset(one_i[:], 1)
            ve.memset(rows_all[:, BLOCKS, :], 0.0)
            ve.memset(xT_all[:, BLOCKS, :], 0.0)
            ve.memset(pe_tab[:], 0)
            ve.memset(ve_tab[:], 0).then_inc(made_v, 1)
            ve.wait_ge(made, POOL_CONSTANTS)
            ve.wait_ge(made_v, 2)
            ve.tensor_copy(slot_f[:], slot_i[:]).then_inc(made_v, 1)
            ve.tensor_copy(item_f[:], item_i[:])
            ve.tensor_copy(lane_f[:], lane_i[:])
            ve.tensor_copy(code_f[:], code_i[:])
            ve.tensor_copy(edge_f[:, 0:1], edge_i[:])
            ve.tensor_scalar(edge_f[:, 1:2], edge_i[:], float(P), None, ALU.add)
            ve.tensor_tensor(bit_i[:], one_i[:], lane_i[:], ALU.logical_shift_left)
            ve.tensor_tensor(has_i[:], code_i[:, None, :].broadcast_to([P, E, PAIRS]),
                             lane_i[:, :, None].broadcast_to([P, E, PAIRS]), ALU.logical_shift_right)\
                .then_inc(made_v, 1)
            ve.wait_ge(made_v, 4)
            ve.tensor_scalar(has_i[:], has_i[:], 1, None, ALU.bitwise_and)
            ve.tensor_copy(bit_f[:], bit_i[:]).then_inc(made_v, 1)
            ve.wait_ge(made_v, 5)
            ve.tensor_copy(has_f[:], has_i[:]).then_inc(made_v, 1)
            ve.wait_ge(made_v, 6)

            def row_max(b):
                ve.wait_ge(s_ready, (b + 1).number)
                ve.tensor_reduce(nmax[:, b.half, :], s_ps, X, ALU.max, negate=True).then_inc(nmax_ready, 1)

            def choose_a(b):
                if isinstance(b.quarter, int) and b.number == 0:
                    ve.wait_ge(logit_ready, 1)
                for c in range(C):
                    ins = ve.max(top[:, b.half, c, :], logit_ps[:, c, :])
                ins.then_inc(top_ready, 1)

            def choose_b(b):
                ve.wait_ge(top_ready, (b + 1).number)
                ve.tensor_tensor(shifted[:, b.half], logit_ps,
                                 top[:, b.half, :, 0:1].broadcast_to([P, C, E]), ALU.subtract)\
                    .then_inc(shifted_ready, 1)
                for c in range(C):
                    ins = ve.max_index(best[:, b.half, c, :], top[:, b.half, c, :], logit_ps[:, c, :])
                ins.then_inc(best_ready, 1)

            def choose_c(b):
                ve.wait_ge(best_ready, (b + 1).number)
                ve.tensor_tensor(onehot[:, b.slot], lane_f[:, None, None, :].broadcast_to([P, C, K, E]),
                                 best[:, b.half, :, 0:K, None].broadcast_to([P, C, K, E]),
                                 ALU.is_equal).then_inc(onehot_ready, 1)

            def choose_d(b):
                ve.wait_ge(onehot_ready, (b + 1).number)
                ve.tensor_tensor(bits[:], onehot[:, b.slot], bit_f[:, None, None, :].broadcast_to([P, C, K, E]),
                                 ALU.mult).then_inc(bits_ready, 1)

            def choose_e(b):
                ve.wait_ge(bits_ready, (b + 1).number)
                ve.tensor_reduce(code[:], bits[:].rearrange("p c k e -> p c (k e)"), X, ALU.add)\
                    .then_inc(code_ready, 1)

            def choose_f(b):
                ve.wait_ge(code_ready, (b + 1).number)
                ve.tensor_tensor(pairhot[:, b.slot], code_f[:, None, :].broadcast_to([P, C, PAIRS]),
                                 code[:, :, None].broadcast_to([P, C, PAIRS]), ALU.is_equal)\
                    .then_inc(pairhot_ready, 1)

            def see(b):
                ve.wait_ge(pairhot_ready, (b + 1).number)
                at = 2 * b.half
                ve.tensor_tensor(seen[:, at + 1], seen[:, at], pairhot[:, b.slot, 0], ALU.add)\
                    .then_inc(seen_ready, 1)
                ve.wait_ge(seen_ready, b.number * C + 1)
                ve.tensor_tensor(seen[:, (at + 2) % 4], seen[:, at + 1], pairhot[:, b.slot, 1], ALU.add)\
                    .then_inc(seen_ready, 1)

            def place_a(b):
                ve.wait_ge(rank_ready, (b + 1).number)
                if (b + 1).valid(BATCHES):
                    ve.wait_ge(logit_ready, (b + 2).number)
                ve.tensor_tensor(picked[:], rank_ps, pairhot[:, b.slot], ALU.mult).then_inc(picked_ready, 1)

            def place_b(b):
                ve.wait_ge(picked_ready, (b + 1).number)
                ve.tensor_reduce(rank_all[:, bass.ds(b.number * C, C)], picked[:], X, ALU.add)\
                    .then_inc(ranked, 1)

            def invert_total(b):
                ve.wait_ge(expd_ready, (b + 1).number * C)
                ve.reciprocal(rtotal[:, b.slot], total[:, b.slot]).then_inc(rtotal_ready, 1)

            def residual_a(b):
                ve.reciprocal(rinv[:, b.half], psum_[:, b.half]).then_inc(rinv_ready, 1)

            def residual(b):
                ve.wait_ge(rinv_ready, (b + 1).number)
                ve.wait_ge(o_ready, (b + 1).number)
                ve.wait_ge(x_loaded[b.slot], 16 * (b.turn + 1))
                for c in range(C):
                    ins = ve.scalar_tensor_tensor(out=hid[:, b.half, c, :], in0=o_ps[:, c, :],
                                                  scalar=rinv[:, b.half, c:c + 1],
                                                  in1=xin[:, b.slot, c, :], op0=ALU.mult, op1=ALU.add)
                ins.then_inc(hid_ready, 1)

            def statistics(b):
                ve.wait_ge(hid_ready, (b + 1).number)
                for c in range(C):
                    ve.bn_stats(stats[:, c, :], hid[:, b.half, c, :]).then_inc(stats_ready, 1)

            def aggregate(b):
                for c in range(C):
                    ve.bn_aggr(mv[:, b.half, c, :], stats[:, c, :]).then_inc(mv_ready, 1)

            def keep_pT(b):
                ve.wait_ge(pT_ready, (b + 1).number)
                ve.tensor_copy(probT[:, b.half, 1, :], pT_ps[1]).then_inc(pT1_kept, 1)

            def normalise(b):
                ve.wait_ge(rstd_ready, (b + 1).number)
                wait(ve, rows_stored[b.slot], b.turn * 16)
                for c in range(C):
                    ins = ve.tensor_scalar(x1[:, b.slot, c, 0:D], hid[:, b.half, c, :],
                                           mv[:, b.half, c, 0:1], rstd[:, b.half, c:c + 1],
                                           ALU.subtract, ALU.mult)
                ins.then_inc(x1_ready, 1)

            def step(i):
                if (i - 1).valid(BATCHES):
                    row_max(i - 1)
                if (i - 3).valid(BATCHES):
                    normalise(i - 3)
                if (i - 2).valid(BATCHES):
                    residual_a(i - 2)
                    residual(i - 2)
                if (i - 5).valid(BATCHES):
                    place_a(i - 5)
                if (i - 4).valid(BATCHES):
                    choose_a(i - 4)
                if (i - 4).valid(BATCHES):
                    choose_b(i - 4)
                if (i - 2).valid(BATCHES):
                    statistics(i - 2)
                if (i - 4).valid(BATCHES):
                    choose_c(i - 4)
                if (i - 5).valid(BATCHES):
                    place_b(i - 5)
                if (i - 4).valid(BATCHES):
                    choose_d(i - 4)
                if (i - 4).valid(BATCHES):
                    choose_e(i - 4)
                if (i - 5).valid(BATCHES):
                    invert_total(i - 5)
                if (i - 4).valid(BATCHES):
                    choose_f(i - 4)
                if (i - 2).valid(BATCHES):
                    ve.wait_ge(stats_ready, (i - 1).number * C)
                if (i - 1).valid(BATCHES):
                    keep_pT(i - 1)
                if (i - 2).valid(BATCHES):
                    aggregate(i - 2)
                if (i - 4).valid(BATCHES):
                    see(i - 4)

            steps(ve, *WHOLE, LAST, step)

            made_steps = [0]

            def tabled(ins):
                made_steps[0] += 1
                ins.then_inc(table, 1)
                ve.wait_ge(table, made_steps[0])

            ve.wait_ge(count_ready, 1)
            tabled(ve.tensor_copy(count[:], bank[6][:, 0:PAIRS]))
            tabled(ve.tensor_tensor_scan(upto[:], count[:], zeros[:], 0.0, ALU.add, ALU.add))
            tabled(ve.tensor_tensor(start[:], upto[:], count[:], ALU.subtract))

            ve.wait_ge(pairs_kept, BATCHES)
            ve.wait_ge(ranked, BATCHES)
            tabled(ve.tensor_tensor(started[:], pairhot_all[:], start[:, None, :].broadcast_to([P, TILES, PAIRS]),
                                    ALU.mult))
            tabled(ve.tensor_reduce(pos_f[:], started[:], X, ALU.add))
            tabled(ve.tensor_tensor(pos_i[:], pos_f[:], rank_all[:], ALU.add))
            ve.tensor_scalar(posblk_i[:], pos_i[:], P.bit_length() - 1, None, ALU.logical_shift_right)
            tabled(ve.tensor_scalar(posrow_i[:], pos_i[:], P - 1, None, ALU.bitwise_and))
            ve.tensor_copy(posblk[:], posblk_i[:]).then_inc(pos_ready, 1)
            tabled(ve.tensor_copy(posrow[:], posrow_i[:]))
            for g in range(TILES // GROUP):
                wait(ve, group_done, g - 1)
                ve.tensor_tensor(rowhot[:, g % 2], item_f[:, None, 0:P].broadcast_to([P, GROUP, P]),
                                 posrow[:, g * GROUP:(g + 1) * GROUP, None].broadcast_to([P, GROUP, P]),
                                 ALU.is_equal).then_inc(rowhot_ready, 1)
            ve.wait_ge(group_done, TILES // GROUP)
            tabled(ve.tensor_copy(sorted_f[:], bank[2][:, 0:BLOCKS]))

            def aim(n):
                ve.tensor_scalar(aim_at[:, n.slot, :], sorted_f[:, bass.ds(n.number, 1)], 1.0, None, ALU.mult)\
                    .then_inc(aimed, 1)

            for n in range(4):
                aim(At(0, n))

            tabled(ve.tensor_scalar(below[:], start[0:BLOCKS], edge_f[0:BLOCKS, 1:2], None, ALU.is_lt))
            tabled(ve.scalar_tensor_tensor(out=inside[:], in0=upto[0:BLOCKS], scalar=edge_f[0:BLOCKS, 0:1],
                                           in1=below[:], op0=ALU.is_gt, op1=ALU.mult))
            tabled(ve.tensor_tensor(among[:], has_f[0:BLOCKS], inside[:, None, :].broadcast_to([BLOCKS, E, PAIRS]),
                                    ALU.mult))
            tabled(ve.tensor_reduce(active[:], among[:], X, ALU.max))
            ve.tensor_tensor_scan(scan[:], active[:], zeros[0:BLOCKS, 0:E], 0.0, ALU.add, ALU.add)\
                .then_inc(scan_ready, 1)
            ve.wait_ge(scan_ready, 1)
            ve.wait_ge(blocks_before, 1)
            tabled(ve.tensor_tensor(cells[:], scan[:], bank[0][0:BLOCKS, 0:1].broadcast_to([BLOCKS, E]), ALU.add))
            tabled(ve.tensor_tensor(past[:], cells[:, None, :].broadcast_to([BLOCKS, ITEMS, E]),
                                    item_f[0:BLOCKS, :, None].broadcast_to([BLOCKS, ITEMS, E]), ALU.is_le))
            with nc.allow_low_precision(reason="counts up to 8"):
                ve.tensor_reduce(npast[:], past[:], X, ALU.add).then_inc(npast_ready, 1)
            ve.wait_ge(cells_ready, 1)
            tabled(ve.tensor_copy(cell_i[:], bank[1][0:1, 0:ITEMS]))
            ve.tensor_scalar(act_tab[:], cell_i[:], E - 1, WE.bit_length() - 1,
                             ALU.bitwise_and, ALU.logical_shift_left).then_inc(items_known, 1)
            ve.tensor_scalar(exp_i[:], cell_i[:], E - 1, None, ALU.bitwise_and)
            tabled(ve.tensor_scalar(blk_i[:], cell_i[:], E.bit_length() - 1, None, ALU.logical_shift_right))
            ve.tensor_copy(pe_tab[:, 2:, 0], act_tab[:])
            ve.tensor_scalar(pe_tab[:, 0:ITEMS, 1], blk_i[:], float(P), None, ALU.mult).then_inc(items_known, 1)
            tabled(ve.tensor_scalar(ve_tab[:, 2:, 0], blk_i[:], float(ROW), None, ALU.mult))
            tabled(ve.scalar_tensor_tensor(out=ve_tab[:, 2:, 1], in0=exp_i[:], scalar=float(D),
                                           in1=ve_tab[:, 2:, 0], op0=ALU.add, op1=ALU.add))

            def multiply(m, k):
                ve.wait_ge(act_ready, m.number * 2 + (k + 1))
                ve.tensor_tensor(gated[:, 2 * m.half + k], act1[:, k], h_ps[k][:, HC * P:2 * HC * P], ALU.mult)\
                    .then_inc(gated_ready, 1)

            def add_up(m, k, column, score):
                ve.wait_ge(y_ready, m.number * 2 + (k + 1))
                wait(ve, summed, m.number * 2 + k)
                rows = rows_flat[:, bass.ds(column, D)]
                ve.scalar_tensor_tensor(out=rows, in0=y_ps[2 * m.half + k][:, 0:D],
                                        scalar=rows_flat[:, bass.ds(score, 1)], in1=rows,
                                        op0=ALU.mult, op1=ALU.add).then_inc(summed, 1)

            def statistics2(f):
                if f.valid(BLOCKS) and isinstance(f.quarter, int) and f.number + DONE_LAG > STEPS:
                    ve.wait_ge(summed, ITEMS)
                else:
                    ve.wait_ge(summed, (f + DONE_LAG).number * 2)
                ve.bn_stats(stats2[:, f.half, :], rows_all[:, bass.ds(f.number, 1), 0:D].rearrange("p o d -> p (o d)"))\
                    .then_inc(stats2_ready, 1)

            def finish(f):
                ve.wait_ge(rstd2_ready, (f + 1).number)
                wait(ve, stored[f.slot], f.turn * 16)
                ve.tensor_scalar(token[:, f.slot, :], rows_flat[:, bass.ds(f.number * ROW + TAG, 1)], 1.0, None,
                                 ALU.mult)
                ve.tensor_scalar(res[:, f.slot, :], rows_flat[:, bass.ds(f.number * ROW, D)],
                                 mv2[:, f.slot, 0:1], rstd2[:, f.slot, :], ALU.subtract, ALU.mult)\
                    .then_inc(res_ready, 1)

            def aggregate2(f):
                ve.bn_aggr(mv2[:, f.slot, :], stats2[:, f.half, :]).then_inc(mv2_ready, 1)

            items = [ve.alloc_register(f"item{k}_{what}") for k in range(2) for what in ("column", "score")]

            def step2(m):
                if (m - 1).valid(STEPS):
                    value = load_values(ve, items, ve_tab[:].rearrange("o i j -> o (i j)")[
                        0:1, bass.ds(m.number * 4, 4)], [TOP_COLUMN, TOP_COLUMN + ROW - 1] * 2)
                for k in range(2):
                    if m.valid(STEPS):
                        multiply(m, k)
                    if k == 0 and (m + 4).valid(BLOCKS):
                        aim(m + 4)
                    if (m - 1).valid(STEPS):
                        add_up(m - 1, k, value[2 * k], value[2 * k + 1])
                if (m - DONE_LAG).valid(BLOCKS):
                    statistics2(m - DONE_LAG)
                    ve.wait_ge(stats2_ready, (m - DONE_LAG + 1).number)
                if (m - DONE_LAG - 1).valid(BLOCKS):
                    finish(m - DONE_LAG - 1)
                if (m - DONE_LAG).valid(BLOCKS):
                    aggregate2(m - DONE_LAG)

            steps(ve, *WHOLE2, LAST2, step2)


_INS = ["L0_attn_x", "L0_attn_W_qkv", "L0_ffn_gate_w", "L0_ffn_w1", "L0_ffn_w2", "L0_ffn_w3"]


def kernel(**inputs):
    import numpy as _np
    import concourse.bacc as _bacc
    from concourse import mybir as _mybir
    from concourse.bass_utils import run_bass_kernel_spmd as _run

    nc = _bacc.Bacc("TRN2", target_bir_lowering=False, num_devices=1)
    arrays, args = {}, []
    for name in _INS:
        a = _np.ascontiguousarray(inputs[name])
        arrays[f"in_{name}_dram"] = a
        args.append(nc.dram_tensor(f"in_{name}_dram", a.shape, _mybir.dt.from_np(a.dtype), kind="ExternalInput").ap())
    shape = inputs["L0_attn_x"].shape
    args.append(nc.dram_tensor("out_0_dram", shape, _mybir.dt.float32, kind="ExternalOutput").ap())
    attention_moe(nc, *args)
    r = _run(nc, [arrays], core_ids=[0])
    return r.results[0]["out_0_dram"]
```

```python
from contextlib import ExitStack

import concourse.bass as bass
from concourse import mybir

F32 = mybir.dt.float32
BF16 = mybir.dt.bfloat16
I32 = mybir.dt.int32
U32 = mybir.dt.uint32
ALU = mybir.AluOpType
ACT = mybir.ActivationFunctionType
X = mybir.AxisListType.X

P = 128
EPS = 1e-5


class At:

    def __init__(self, quarter, offset):
        self.quarter, self.offset = quarter, offset

    def __add__(self, n):
        return At(self.quarter, self.offset + n)

    def __sub__(self, n):
        return At(self.quarter, self.offset - n)

    @property
    def number(self):
        return self.quarter * 4 + self.offset

    @property
    def slot(self):
        return self.offset % 4

    @property
    def half(self):
        return self.offset % 2

    @property
    def turn(self):
        return self.quarter + self.offset // 4

    def valid(self, count):
        return not isinstance(self.quarter, int) or 0 <= self.number < count


def wait(engine, semaphore, value):
    if not isinstance(value, int) or value > 0:
        engine.wait_ge(semaphore, value)


def steps(engine, first_whole, last_whole, last, step):
    turns = (last_whole + 1 - first_whole) // 4
    for n in range(first_whole):
        step(At(0, n))
    with engine.Fori(0, turns) as turn:
        for n in range(4):
            step(At(turn, first_whole + n))
    for n in range(first_whole + 4 * turns, last + 1):
        step(At(0, n))


def pair_path(experts):
    path, start = [], 1
    for a in range(experts - 1):
        rest = [b for b in range(a + 1, experts) if b != start]
        path += [(a, b) for b in [start] + rest]
        start = path[-1][1] if path[-1][1] > a + 1 else experts - 1
    assert len(set(path)) == experts * (experts - 1) // 2
    assert all(set(p) & set(q) for p, q in zip(path, path[1:]))
    return path


def attention_moe(nc, x, w_qkv, gate_w, w1, w2, w3, out):
    BATCHES, N, D = x.shape
    E, _, H = w1.shape
    C = N // P
    TILES = BATCHES * C
    TOKENS = BATCHES * N
    K = 2
    HC = H // P
    PATH = pair_path(E)
    PAIRS = len(PATH)
    ROW = D + E
    BLOCKS = TOKENS // P
    ITEMS = (K * BLOCKS + PAIRS - 1 + 1) // 2 * 2
    DONE_LAG = PAIRS // 2 + 1
    GROUP = 8
    SCALE = float(D) ** -0.5
    WE = 2 * H
    assert D == P and N == 2 * P and H == 2 * P and BATCHES % 4 == 0 and BLOCKS % 4 == 0 and BLOCKS <= P
    assert K * BLOCKS + PAIRS - 1 <= ITEMS and TILES % GROUP == 0
    POOL_TILES = TILES * 3 // 8
    assert 2 * DONE_LAG >= K + PAIRS - 1

    x_tiles = x.rearrange("b (c p) d -> b p c d", p=P)
    out_rows = out.rearrange("b n d -> (b n) d")
    rows_dram = nc.dram_tensor("rows", [TOKENS, ROW], F32, kind="Internal").ap()
    row_tiles = rows_dram.rearrange("(b c p) r -> b p c r", p=P, c=C)

    with ExitStack() as ctx:
        def sb(name, shape, dt=F32):
            return ctx.enter_context(nc.sbuf_tensor(name, shape, dt))

        def sem(name):
            return ctx.enter_context(nc.semaphore(name))

        def sems(name, n):
            return [sem(f"{name}{i}") for i in range(n)]

        ident = sb("ident", [P, P])
        before = sb("before", [P, P], BF16)
        ones = sb("ones", [P, P], BF16)
        expert_i = sb("expert_i", [P, E], I32)
        expert_f = sb("expert_f", [P, E])
        one_i = sb("one_i", [P, E], I32)
        bit_i = sb("bit_i", [P, E], I32)
        bit_f = sb("bit_f", [P, E])
        code_i = sb("code_i", [P, PAIRS], I32)
        code_f = sb("code_f", [P, PAIRS])
        has_i = sb("has_i", [P, E, PAIRS], I32)
        has_f = sb("has_f", [P, E, PAIRS])
        item_i = sb("item_i", [P, ITEMS], I32)
        item_f = sb("item_f", [P, ITEMS])
        edge_i = sb("edge_i", [P, 1], I32)
        lane_i = sb("lane_i", [P, 1], I32)
        edge_f = sb("edge_f", [P, 2])
        eps_col = sb("eps_col", [P, C])
        minus_half = sb("minus_half", [P, C])
        var = sb("var", [P, C])
        zeros = sb("zeros", [P, PAIRS])
        w_in = sb("w_in", [P, 3, D])
        wqk = sb("wqk", [P, D])
        wvT = sb("wvT", [P, D])
        gate_in = sb("gate_in", [E, D])
        gateT = sb("gateT", [P, E])
        w13 = sb("w13", [P, E, 2, H])
        w2s = sb("w2s", [P, E, WE])

        xin = sb("xin", [P, 4, C, D])
        xT = sb("xT", [P, 2, N])
        yv = sb("yv", [P, 2, 2, N])
        nmax = sb("nmax", [P, 2, C])
        prob = sb("prob", [P, 2, C, N])
        psum_ = sb("psum_", [P, 2, C])
        rinv = sb("rinv", [P, 2, C])
        probT = sb("probT", [P, 2, C, N])
        hid = sb("hid", [P, 2, C, D])
        stats = sb("stats", [P, C, 6])
        mv = sb("mv", [P, 2, C, 2])
        rstd = sb("rstd", [P, 2, C])
        x1 = sb("x1", [P, 4, C, ROW])
        x1T = sb("x1T", [P, 2, N])
        top = sb("top", [P, 2, C, 8])
        best = sb("best", [P, 2, C, 8], U32)
        shifted = sb("shifted", [P, 2, C, E])
        onehot = sb("onehot", [P, 4, C, K, E])
        bits = sb("bits", [P, C, K, E])
        code = sb("code", [P, C])
        pairhot = sb("pairhot", [P, 4, C, PAIRS], BF16)
        seen = sb("seen", [P, 4, PAIRS], BF16)
        picked = sb("picked", [P, C, PAIRS])
        pairhot_all = sb("pairhot_all", [P, TILES, PAIRS], BF16)
        rank_all = sb("rank_all", [P, TILES])
        expd = sb("expd", [P, 4, C, E])
        total = sb("total", [P, 4, C])
        rtotal = sb("rtotal", [P, 4, C])
        chosen = sb("chosen", [P, C, E])
        weight = sb("weight", [P, C, E])

        count = sb("count", [P, PAIRS])
        upto = sb("upto", [P, PAIRS])
        start = sb("start", [P, PAIRS])
        started = sb("started", [P, TILES, PAIRS])
        pos_f = sb("pos_f", [P, TILES])
        pos_i = sb("pos_i", [P, TILES], I32)
        posrow_i = sb("posrow_i", [P, TILES], I32)
        posrow = sb("posrow", [P, TILES])
        posblk_i = sb("posblk_i", [P, TILES], I32)
        posblk = sb("posblk", [P, TILES])
        rowhot = sb("rowhot", [P, 2, GROUP, P], BF16)
        blkhot = sb("blkhot", [P, 2, GROUP, BLOCKS], BF16)
        blktok = sb("blktok", [P, 2, GROUP, 2, BLOCKS], BF16)
        tiles_bf = sb("tiles_bf", [P, TILES], BF16)
        lane_f = sb("lane_f", [P, 1])
        sorted_f = sb("sorted_f", [P, BLOCKS])
        below = sb("below", [BLOCKS, PAIRS])
        inside = sb("inside", [BLOCKS, PAIRS])
        among = sb("among", [BLOCKS, E, PAIRS])
        active = sb("active", [BLOCKS, E])
        scan = sb("scan", [BLOCKS, E], BF16)
        cells = sb("cells", [BLOCKS, E])
        past = sb("past", [BLOCKS, ITEMS, E])
        npast = sb("npast", [BLOCKS, ITEMS], BF16)
        cell_i = sb("cell_i", [1, ITEMS], I32)
        blk_i = sb("blk_i", [1, ITEMS], I32)
        exp_i = sb("exp_i", [1, ITEMS], I32)
        pe_tab = sb("pe_tab", [1, ITEMS + 4, 2], I32)
        ve_tab = sb("ve_tab", [1, ITEMS + 4, 2], I32)
        act_tab = sb("act_tab", [1, ITEMS + 2], I32)

        rows_all = sb("rows_all", [P, BLOCKS + 1, ROW])
        xT_all = sb("xT_all", [P, BLOCKS + 1, P])
        row_in = sb("row_in", [P, 4, ROW])
        w_now = sb("w_now", [P, 2, WE])
        act1 = sb("act1", [P, 2, HC * P])
        gated = sb("gated", [P, 4, HC * P])
        stats2 = sb("stats2", [P, 2, 6])
        mv2 = sb("mv2", [P, 4, 2])
        rstd2 = sb("rstd2", [P, 4, 1])
        res = sb("res", [P, 4, D])
        token = sb("token", [P, 4, 1], U32)
        aim_at = sb("aim_at", [P, 4, 1], U32)
        rows_flat = rows_all[:].rearrange("p b r -> p (b r)")
        xT_flat = xT_all[:].rearrange("p b t -> p (b t)")
        w13_flat = w13[:].rearrange("p e j h -> p (e j h)")
        w2_flat = w2s[:].rearrange("p e c -> p (e c)")

        bank = [ctx.enter_context(nc.psum_tensor(f"bank{i}", [P, 512], F32)) for i in range(8)]
        xT_ps = bank[0][:, 0:N]
        yv_ps = bank[1][:, :]
        s_ps = bank[2][:, :].rearrange("p (c n) -> p c n", c=C)
        pT_ps = bank[3][:, :].rearrange("p (m n) -> p m n", m=C)
        o_ps = bank[4][:, 0:C * D].rearrange("p (c d) -> p c d", c=C)
        x1T_ps = bank[5][:, 0:N]
        logit_ps = bank[6][:, 0:C * E].rearrange("p (c e) -> p c e", c=C)
        rank_ps = bank[4][:, C * D:C * D + C * PAIRS].rearrange("p (c e) -> p c e", c=C)
        h_ps = [bank[0], bank[1]]
        y_ps = [bank[2], bank[3], bank[4], bank[5]]
        blkT_ps = [bank[6], bank[7]]

        w_loaded = sem("w_loaded")
        e_loaded = sem("e_loaded")
        made = sem("made")
        made_v = sem("made_v")
        prep_ps = sem("prep_ps")
        prep_sb = sem("prep_sb")
        x_loaded = sems("x_loaded", 4)
        xT_ready = sem("xT_ready")
        xT_kept = sem("xT_kept")
        yv_ready = sem("yv_ready")
        yv_kept = sem("yv_kept")
        s_ready = sem("s_ready")
        nmax_ready = sem("nmax_ready")
        prob_ready = sem("prob_ready")
        pT_ready = sem("pT_ready")
        pT_kept = sem("pT_kept")
        o_ready = sem("o_ready")
        hid_ready = sem("hid_ready")
        rinv_ready = sem("rinv_ready")
        stats_ready = sem("stats_ready")
        mv_ready = sem("mv_ready")
        var_ready = sem("var_ready")
        var2_ready = sem("var2_ready")
        rstd_ready = sem("rstd_ready")
        x1_ready = sem("x1_ready")
        x1T_ready = sem("x1T_ready")
        x1T_kept = sem("x1T_kept")
        logit_ready = sem("logit_ready")
        top_ready = sem("top_ready")
        best_ready = sem("best_ready")
        shifted_ready = sem("shifted_ready")
        onehot_ready = sem("onehot_ready")
        bits_ready = sem("bits_ready")
        code_ready = sem("code_ready")
        pairhot_ready = sem("pairhot_ready")
        seen_ready = sem("seen_ready")
        rank_ready = sem("rank_ready")
        picked_ready = sem("picked_ready")
        ranked = sem("ranked")
        expd_ready = sem("expd_ready")
        rtotal_ready = sem("rtotal_ready")
        chosen_ready = sem("chosen_ready")
        weight_ready = sem("weight_ready")
        scored = sem("scored")
        pairs_kept = sem("pairs_kept")
        rows_stored = sems("rows_stored", 4)
        pool_turns = sem("pool_turns")

        count_ready = sem("count_ready")
        table = sem("table")
        rowhot_ready = sem("rowhot_ready")
        blkhot_ready = sem("blkhot_ready")
        start_ready = sem("start_ready")
        started_ready = sem("started_ready")
        tiles_put = sem("tiles_put")
        lanes_put = sem("lanes_put")
        group_done = sem("group_done")
        scan_ready = sem("scan_ready")
        blocks_before = sem("blocks_before")
        npast_ready = sem("npast_ready")
        cells_ready = sem("cells_ready")
        sorted_ready = sem("sorted_ready")
        aimed = sem("aimed")
        token_ready = sem("token_ready")
        items_known = sem("items_known")
        gathered = sems("gathered", 4)
        turned = sem("turned")
        w_placed = sem("w_placed")
        h_ready = sem("h_ready")
        act_ready = sem("act_ready")
        gated_ready = sem("gated_ready")
        y_ready = sem("y_ready")
        summed = sem("summed")
        stats2_ready = sem("stats2_ready")
        mv2_ready = sem("mv2_ready")
        rstd2_ready = sem("rstd2_ready")
        res_ready = sem("res_ready")
        stored = sems("stored", 4)

        POOL_CONSTANTS = 11 + PAIRS

        WHOLE = (6, 29)
        LAST = BATCHES - 1 + 5
        STEPS = ITEMS // 2
        WHOLE2 = (DONE_LAG + 5, BLOCKS - 5)
        assert WHOLE2[0] % 2 == 0
        LAST2 = BLOCKS - 1 + DONE_LAG + 4

        def load_values(engine, registers, table, tops):
            engine.load(registers, table)
            return [nc.s_assert_within(engine.snap(r), 0, top, skip_runtime_bounds_check_because=
                                       "an item's expert is below E, its block at most BLOCKS")
                    for r, top in zip(registers, tops)]

        TOP_EXPERT = (E - 1) * WE
        TOP_BLOCK = BLOCKS * P
        TOP_COLUMN = BLOCKS * ROW

        block = ctx.enter_context(nc.Block())

        @block.sync
        def _(sp):
            sp.dma_start(w_in[:], w_qkv.rearrange("(j e) d -> e j d", e=P)).then_inc(w_loaded, 16)
            sp.dma_start(gate_in[:], gate_w).then_inc(w_loaded, 16)

            def load(b):
                wait(sp, hid_ready, (b - 3).number)
                sp.dma_start(xin[:, b.slot], x_tiles[b.number]).then_inc(x_loaded[b.slot], 16)

            def keep(b):
                sp.wait_ge(scored, (b + 1).number)
                sp.dma_start(row_tiles[b.number], x1[:, b.slot]).then_inc(rows_stored[b.slot], 16)

            def step(i):
                if (i + 2).valid(BATCHES):
                    load(i + 2)
                if (i - 5).valid(BATCHES):
                    keep(i - 5)
                if isinstance(i.quarter, int) and i.number == 2:
                    sp.dma_start(w13[:, :, 0, :], w1.rearrange("e d h -> d e h")).then_inc(e_loaded, 16)
                if isinstance(i.quarter, int) and i.number == 4:
                    sp.dma_start(w13[:, :, 1, :], w3.rearrange("e d h -> d e h")).then_inc(e_loaded, 16)
                if isinstance(i.quarter, int) and i.number == 5:
                    for c in range(HC):
                        sp.dma_start(w2s[:, :, c * D:(c + 1) * D],
                                     w2.rearrange("e (c h) d -> c h e d", h=P)[c]).then_inc(e_loaded, 16)

            load(At(0, 0))
            load(At(0, 1))
            steps(sp, *WHOLE, LAST, step)

        @block.gpsimd
        def _(pool):
            pool.memset(ident[:], 0.0).then_inc(made, 1)
            pool.wait_ge(made, 1)
            pool.affine_select(out=ident[:], in_=ident[:], compare_op=ALU.not_equal, fill=1.0,
                               base=0, pattern=[[-1, P]], channel_multiplier=1).then_inc(made, 1)
            pool.memset(before[:], 1.0).then_inc(made, 1)
            pool.memset(ones[:], 1.0).then_inc(made, 1)
            pool.wait_ge(made, 3)
            pool.affine_select(out=before[:], in_=before[:], compare_op=ALU.is_gt, fill=0.0,
                               base=0, pattern=[[1, P]], channel_multiplier=-1).then_inc(made, 1)
            pool.iota(expert_i[:], [[1, E]], 0, 0).then_inc(made, 1)
            pool.iota(item_i[:], [[1, ITEMS]], 0, 0).then_inc(made, 1)
            pool.iota(edge_i[:], [[0, 1]], 0, P).then_inc(made, 1)
            pool.iota(lane_i[:], [[0, 1]], 0, 1).then_inc(made, 1)
            pool.memset(eps_col[:], EPS).then_inc(made, 1)
            pool.memset(minus_half[:], -0.5).then_inc(made, 1)
            for q, (a, b) in enumerate(PATH):
                pool.memset(code_i[:, q:q + 1], (1 << a) + (1 << b)).then_inc(made, 1)

            def deviation(b):
                pool.wait_ge(mv_ready, (b + 1).number * C)
                pool.tensor_tensor(var[:, 0:C], mv[:, b.half, :, 1], eps_col[:, 0:C], ALU.add).then_inc(var_ready, 1)
                pool.wait_ge(var_ready, (b + 1).number)
                pool.tensor_tensor(rstd[:, b.half, :], var[:, 0:C], minus_half[:, 0:C], ALU.pow)\
                    .then_inc(rstd_ready, 1)

            def score_rows(b):
                pool.wait_ge(rtotal_ready, (b + 1).number)
                pool.tensor_tensor(chosen[:], onehot[:, b.slot, :, 0, :], onehot[:, b.slot, :, 1, :], ALU.add)\
                    .then_inc(chosen_ready, 1)
                pool.wait_ge(chosen_ready, (b + 1).number)
                pool.tensor_tensor(weight[:], chosen[:], expd[:, b.slot], ALU.mult).then_inc(weight_ready, 1)
                pool.wait_ge(weight_ready, (b + 1).number)
                pool.tensor_tensor(x1[:, b.slot, :, D:D + E], weight[:],
                                   rtotal[:, b.slot, :, None].broadcast_to([P, C, E]), ALU.mult)\
                    .then_inc(scored, 1)

            def see(b):
                pool.wait_ge(pairhot_ready, (b + 1).number)
                at = 2 * b.half
                pool.tensor_tensor(seen[:, at + 1], seen[:, at], pairhot[:, b.slot, 0], ALU.add)\
                    .then_inc(seen_ready, 1)
                pool.wait_ge(seen_ready, b.number * C + 1)
                pool.tensor_tensor(seen[:, (at + 2) % 4], seen[:, at + 1], pairhot[:, b.slot, 1], ALU.add)\
                    .then_inc(seen_ready, 1)

            def keep_pairs(b):
                pool.tensor_tensor(pairhot_all[:, bass.ds(b.number * C, C), :], pairhot[:, b.slot],
                                   pairhot[:, b.slot], ALU.mult).then_inc(pairs_kept, 1)

            def step(i):
                if (i - 2).valid(BATCHES):
                    deviation(i - 2)
                if (i - 4).valid(BATCHES):
                    see(i - 4)
                if (i - 5).valid(BATCHES):
                    score_rows(i - 5)
                    keep_pairs(i - 5)

            pool.wait_ge(made, POOL_CONSTANTS)
            pool.wait_ge(made_v, 1)
            steps(pool, *WHOLE, LAST, step)

            pool.wait_ge(start_ready, 1)
            pool.wait_ge(pairs_kept, BATCHES)
            pool.tensor_tensor(started[:, 0:POOL_TILES], pairhot_all[:, 0:POOL_TILES],
                               start[:, None, :].broadcast_to([P, POOL_TILES, PAIRS]), ALU.mult)\
                .then_inc(started_ready, 1)

            for g in range(TILES // GROUP):
                pool.wait_ge(blkhot_ready, g + 1)
                pool.tensor_tensor(blktok[:, g % 2, :, 0, :], blkhot[:, g % 2],
                                   tiles_bf[:, g * GROUP:(g + 1) * GROUP, None].broadcast_to([P, GROUP, BLOCKS]),
                                   ALU.mult).then_inc(tiles_put, 1)
            for s in range(4):
                pool.wait_ge(rows_stored[s], BATCHES // 4 * 16)

            def gather(n):
                pool.wait_ge(aimed, (n + 1).number)
                pool.sem_inc(pool_turns)
                pool.indirect_dma_start(
                    out=row_in[:, n.slot, :], out_offset=None, in_=rows_dram,
                    in_offset=bass.IndirectOffsetOnAxis(ap=aim_at[:, n.slot, :], axis=0))\
                    .then_inc(gathered[n.slot], 16)

            def deviation2(f):
                pool.wait_ge(mv2_ready, (f + 1).number)
                pool.tensor_tensor(var[:, 0:2], mv2[:, f.slot - 1:f.slot + 1, 1], eps_col[:, 0:2], ALU.add)\
                    .then_inc(var2_ready, 2)
                pool.wait_ge(var2_ready, (f + 1).number)
                pool.tensor_tensor(rstd2[:, f.slot - 1:f.slot + 1, 0], var[:, 0:2], minus_half[:, 0:2], ALU.pow)\
                    .then_inc(rstd2_ready, 2)

            def scatter_out(f):
                pool.wait_ge(token_ready, (f + 1).number)
                pool.wait_ge(res_ready, (f + 1).number)
                pool.sem_inc(pool_turns)
                pool.indirect_dma_start(
                    out=out_rows, in_=res[:, f.slot, :], in_offset=None,
                    out_offset=bass.IndirectOffsetOnAxis(ap=token[:, f.slot, :], axis=0))\
                    .then_inc(stored[f.slot], 16)

            def step2(m):
                if (m + 4).valid(BLOCKS):
                    gather(m + 4)
                if (m - DONE_LAG - 4).valid(BLOCKS):
                    scatter_out(m - DONE_LAG - 4)
                f = m - DONE_LAG - 1
                if f.half == 1 and f.valid(BLOCKS):
                    deviation2(f)

            for n in range(4):
                gather(At(0, n))
            steps(pool, *WHOLE2, LAST2, step2)
            for s in range(4):
                pool.wait_ge(stored[s], BLOCKS // 4 * 16)

        @block.scalar
        def _(act):
            act.preload_act_table(ACT.Exp)
            act.wait_ge(prep_ps, 1)
            act.activation(wqk[:], bank[0][:, 0:D], ACT.Copy, scale=SCALE).then_inc(prep_sb, 1)
            act.wait_ge(prep_ps, 2)
            act.activation(wvT[:], bank[1][:, 0:D], ACT.Copy).then_inc(prep_sb, 1)
            act.wait_ge(prep_ps, 3)
            act.activation(gateT[:], bank[2][:, 0:E], ACT.Copy).then_inc(prep_sb, 1)

            def keep_xT(b):
                act.wait_ge(xT_ready, (b + 1).number)
                act.activation(xT[:, b.half], xT_ps, ACT.Copy).then_inc(xT_kept, 1)

            def keep_yv(b):
                act.wait_ge(yv_ready, (b + 1).number)
                act.activation(yv[:, b.half].rearrange("p j n -> p (j n)"), yv_ps, ACT.Copy)\
                    .then_inc(yv_kept, 1)

            def exponent(b):
                act.wait_ge(nmax_ready, (b + 1).number)
                for c in range(C):
                    act.activation(prob[:, b.half, c, :], s_ps[:, c, :], ACT.Exp,
                                   bias=nmax[:, b.half, c:c + 1],
                                   accum_out=psum_[:, b.half, c:c + 1]).then_inc(prob_ready, 1)

            def keep_pT(b):
                act.wait_ge(pT_ready, (b + 1).number)
                act.activation(probT[:, b.half], pT_ps, ACT.Copy).then_inc(pT_kept, 1)

            def keep_x1T(b):
                act.wait_ge(x1T_ready, (b + 1).number)
                act.activation(x1T[:, b.half], x1T_ps, ACT.Copy).then_inc(x1T_kept, 1)

            def exponent_logits(b):
                act.wait_ge(shifted_ready, (b + 1).number)
                for c in range(C):
                    act.activation(expd[:, b.slot, c, :], shifted[:, b.half, c, :], ACT.Exp,
                                   accum_out=total[:, b.slot, c:c + 1]).then_inc(expd_ready, 1)

            def step(i):
                if (i - 5).valid(BATCHES):
                    exponent_logits(i - 5)
                if (i - 1).valid(BATCHES):
                    exponent(i - 1)
                if i.valid(BATCHES):
                    keep_yv(i)
                if (i - 3).valid(BATCHES):
                    keep_x1T(i - 3)
                if (i - 1).valid(BATCHES):
                    keep_pT(i - 1)
                if (i + 1).valid(BATCHES):
                    keep_xT(i + 1)

            keep_xT(At(0, 0))
            steps(act, *WHOLE, LAST, step)

            act.preload_act_table(ACT.Silu)
            for g in range(TILES // GROUP):
                act.wait_ge(blkhot_ready, g + 1)
                act.activation(blktok[:, g % 2, :, 1, :], blkhot[:, g % 2], ACT.Copy, scale=lane_f[:, 0:1])\
                    .then_inc(lanes_put, 1)

            def keep_block(n):
                act.activation(xT_all[:, bass.ds(n.number, 1), :], blkT_ps[n.half][:, None, 0:P], ACT.Copy)
                act.activation(rows_all[:, bass.ds(n.number, 1), :], row_in[:, n.slot, None, :], ACT.Copy)

            def silu(m, k):
                act.wait_ge(h_ready, (m.number * 2) + (k + 1))
                act.activation(act1[:, k], h_ps[k][:, 0:HC * P], ACT.Silu).then_inc(act_ready, 1)

            def aim(n):
                act.activation(aim_at[:, n.slot, :], sorted_f[:, bass.ds(n.number, 1)], ACT.Copy).then_inc(aimed, 1)

            def address(f):
                act.activation(token[:, f.slot, :], sorted_f[:, bass.ds(f.number, 1)], ACT.Copy)\
                    .then_inc(token_ready, 1)

            def place_w(k, expert):
                act.activation(w_now[:, k], w13_flat[:, bass.ds(expert, WE)], ACT.Copy).then_inc(w_placed, 1)

            experts = [act.alloc_register(f"expert{k}") for k in range(4)]
            expert = []

            def step2(m):
                f = m - DONE_LAG - 3
                if f.valid(BLOCKS):
                    wait(act, stored[f.slot], f.turn * 16)
                for k in range(2):
                    if m.valid(STEPS):
                        silu(m, k)
                    if k == 0 and (m + 4).valid(BLOCKS):
                        aim(m + 4)
                    if k == 0 and m.half == 0 and (m + 1).valid(STEPS):
                        expert[:] = load_values(act, experts, act_tab[0:1, bass.ds((m + 1).number * 2, 4)],
                                                [TOP_EXPERT] * 4)
                    if (m + 1).valid(STEPS):
                        place_w(k, expert[m.half * 2 + k])
                if (m + 2).valid(BLOCKS):
                    keep_block(m + 2)
                if f.valid(BLOCKS):
                    address(f)

            act.wait_ge(sorted_ready, 1)
            for n in range(4):
                aim(At(0, n))
            act.wait_ge(e_loaded, 16 * (2 + HC))
            act.wait_ge(items_known, 1)
            expert[:] = load_values(act, experts, act_tab[0:1, 0:4], [TOP_EXPERT] * 4)
            for k in range(2):
                act.wait_ge(turned, k + 1)
                keep_block(At(0, k))
                place_w(k, expert[k])
            steps(act, *WHOLE2, LAST2, step2)

        @block.tensor
        def _(pe):
            pe.wait_ge(w_loaded, 32)
            pe.wait_ge(made, 2)
            pe.matmul(bank[0][:, 0:D], w_in[:, 0, :], w_in[:, 1, :], start=True, stop=True).then_inc(prep_ps, 1)
            pe.transpose(bank[1][:, 0:D], w_in[:, 2, :], ident[:]).then_inc(prep_ps, 1)
            pe.transpose(bank[2][:, 0:E], gate_in[:, :], ident[0:E, 0:E]).then_inc(prep_ps, 1)
            pe.wait_ge(prep_sb, 3)
            pe.wait_ge(made, 5)
            pe.wait_ge(made_v, 1)

            def turn_x(b):
                pe.wait_ge(x_loaded[b.slot], 16 * (b.turn + 1))
                for c in range(C):
                    ins = pe.transpose(xT_ps[:, c * P:(c + 1) * P], xin[:, b.slot, c, :], ident[:])
                ins.then_inc(xT_ready, 1)

            def project(b):
                pe.wait_ge(xT_kept, (b + 1).number)
                pe.matmul(yv_ps[:, 0:N], wqk[:], xT[:, b.half, :], start=True, stop=True)
                for c in range(C):
                    ins = pe.matmul(yv_ps[:, N + c * D:N + (c + 1) * D], xT[:, b.half, c * P:(c + 1) * P],
                                    wvT[:], start=True, stop=True)
                ins.then_inc(yv_ready, 1)

            def weigh(b):
                pe.wait_ge(pT_kept, (b + 1).number)
                wait(pe, hid_ready, b.number)
                for c in range(C):
                    for m in range(C):
                        ins = pe.matmul(o_ps[:, c, :], probT[:, b.half, m, c * P:(c + 1) * P],
                                        yv[:, b.half, 1, m * D:(m + 1) * D], start=(m == 0), stop=(m == C - 1))
                ins.then_inc(o_ready, 1)

            def turn_x1(b):
                pe.wait_ge(x1_ready, (b + 1).number)
                for c in range(C):
                    ins = pe.transpose(x1T_ps[:, c * P:(c + 1) * P], x1[:, b.slot, c, 0:D], ident[:])
                ins.then_inc(x1T_ready, 1)

            def turn_prob(b):
                pe.wait_ge(prob_ready, (b + 1).number * C)
                for m in range(C):
                    for c in range(C):
                        ins = pe.transpose(pT_ps[:, m, c * P:(c + 1) * P],
                                           prob[:, b.half, c, m * P:(m + 1) * P], ident[:])
                ins.then_inc(pT_ready, 1)

            def score_(b):
                pe.wait_ge(yv_kept, (b + 1).number)
                for c in range(C):
                    ins = pe.matmul(s_ps[:, c, :], yv[:, b.half, 0, c * P:(c + 1) * P], xT[:, b.half, :],
                                    start=True, stop=True)
                ins.then_inc(s_ready, 1)

            def rank(b):
                pe.wait_ge(seen_ready, (b + 1).number * C)
                pe.matmul(rank_ps.rearrange("p c e -> p (c e)"), before[:],
                          pairhot[:, b.slot].rearrange("p c e -> p (c e)"), start=True, stop=False)
                at = 2 * b.half
                pe.matmul(rank_ps.rearrange("p c e -> p (c e)"), ones[:],
                          seen[:, at:at + C].rearrange("p c e -> p (c e)"), start=False, stop=True)\
                    .then_inc(rank_ready, 1)

            def route(b):
                pe.wait_ge(x1T_kept, (b + 1).number)
                wait(pe, best_ready, b.number)
                for c in range(C):
                    ins = pe.matmul(logit_ps[:, c, :], x1T[:, b.half, c * P:(c + 1) * P], gateT[:],
                                    start=True, stop=True)
                ins.then_inc(logit_ready, 1)

            def step(i):
                if (i - 2).valid(BATCHES):
                    weigh(i - 2)
                if (i - 5).valid(BATCHES):
                    if not (i - 2).valid(BATCHES):
                        pe.wait_ge(hid_ready, BATCHES)
                        wait(pe, picked_ready, (i - 5).number)
                    rank(i - 5)
                if i.valid(BATCHES):
                    project(i)
                if (i - 3).valid(BATCHES):
                    turn_x1(i - 3)
                if (i - 1).valid(BATCHES):
                    turn_prob(i - 1)
                if (i + 1).valid(BATCHES):
                    turn_x(i + 1)
                if i.valid(BATCHES):
                    score_(i)
                if (i - 3).valid(BATCHES):
                    route(i - 3)

            turn_x(At(0, 0))
            steps(pe, *WHOLE, LAST, step)
            pe.wait_ge(best_ready, BATCHES)
            pe.matmul(bank[6][:, 0:PAIRS], ones[:], seen[:, 0, :], start=True, stop=True).then_inc(count_ready, 1)
            for g in range(TILES // GROUP):
                pe.wait_ge(rowhot_ready, g + 1)
                pe.wait_ge(tiles_put, g + 1)
                pe.wait_ge(lanes_put, g + 1)
                for t in range(GROUP):
                    tile = g * GROUP + t
                    ins = pe.matmul(bank[2][:, 0:2 * BLOCKS], rowhot[:, g % 2, t, :],
                                    blktok[:, g % 2, t].rearrange("p j b -> p (j b)"),
                                    start=(tile == 0), stop=(tile == TILES - 1))
                ins.then_inc(group_done, 1)
            pe.wait_ge(scan_ready, 1)
            pe.matmul(bank[0][0:BLOCKS, 0:1], before[0:BLOCKS, 0:BLOCKS], scan[:, E - 1:E],
                      start=True, stop=True).then_inc(blocks_before, 1)
            pe.wait_ge(npast_ready, 1)
            pe.matmul(bank[1][0:1, 0:ITEMS], ones[0:BLOCKS, 0:1], npast[:], start=True, stop=True)\
                .then_inc(cells_ready, 1)

            def turn_block(n):
                pe.wait_ge(gathered[n.slot], 16 * (n.turn + 1))
                pe.transpose(blkT_ps[n.half][:, 0:P], row_in[:, n.slot, 0:D], ident[:]).then_inc(turned, 1)

            def up(m, k, column):
                wait(pe, gated_ready, m.number * 2 + (k - 1))
                pe.wait_ge(w_placed, m.number * 2 + (k + 1))
                for c in range(2 * HC):
                    ins = pe.matmul(h_ps[k][:, c * P:(c + 1) * P],
                                    w_now[:, k, c * P:(c + 1) * P],
                                    xT_flat[:, bass.ds(column, P)], start=True, stop=True)
                ins.then_inc(h_ready, 1)

            def down(m, k, expert):
                at = 2 * m.half + k
                for c in range(HC):
                    ins = pe.matmul(y_ps[at][:, 0:D], gated[:, at, c * P:(c + 1) * P],
                                    w2_flat[:, c * D:][:, bass.ds(expert, D)], start=(c == 0), stop=(c == HC - 1))
                ins.then_inc(y_ready, 1)

            items = [pe.alloc_register(f"item{k}_{what}") for k in range(4) for what in ("expert", "column")]
            value = []

            def step2(m):
                if m.half == 0 and m.valid(STEPS + 1):
                    value[:] = load_values(pe, items, pe_tab[:].rearrange("o i j -> o (i j)")[
                        0:1, bass.ds(m.number * 4, 8)], [TOP_EXPERT, TOP_BLOCK] * 4)
                for k in range(2):
                    if m.valid(STEPS):
                        up(m, k, value[4 * m.half + 2 * k + 1])
                    if k == 0 and (m + 2).valid(BLOCKS):
                        turn_block(m + 2)
                    if (m - 1).valid(STEPS):
                        if not m.valid(STEPS):
                            pe.wait_ge(gated_ready, ITEMS - 1 + k)
                        down(m - 1, k, value[4 * m.half + 2 * k])

            turn_block(At(0, 0))
            turn_block(At(0, 1))
            pe.wait_ge(items_known, 2)
            steps(pe, *WHOLE2, LAST2, step2)

        @block.vector
        def _(ve):
            ve.memset(seen[:], 0.0).then_inc(made_v, 1)
            ve.memset(zeros[:], 0.0)
            ve.memset(one_i[:], 1)
            ve.memset(rows_all[:, BLOCKS, :], 0.0)
            ve.memset(xT_all[:, BLOCKS, :], 0.0)
            ve.memset(pe_tab[:], 0)
            ve.memset(act_tab[:], 0)
            ve.memset(ve_tab[:], 0).then_inc(made_v, 1)
            ve.wait_ge(made, POOL_CONSTANTS)
            ve.wait_ge(made_v, 2)
            ve.tensor_copy(item_f[:], item_i[:]).then_inc(made_v, 1)
            ve.tensor_copy(tiles_bf[:], item_i[:, 0:TILES])
            ve.tensor_copy(lane_f[:], lane_i[:])
            ve.tensor_copy(expert_f[:], expert_i[:])
            ve.tensor_copy(code_f[:], code_i[:])
            ve.tensor_copy(edge_f[:, 0:1], edge_i[:])
            ve.tensor_scalar(edge_f[:, 1:2], edge_i[:], float(P), None, ALU.add)
            ve.tensor_tensor(bit_i[:], one_i[:], expert_i[:], ALU.logical_shift_left)
            ve.tensor_tensor(has_i[:], code_i[:, None, :].broadcast_to([P, E, PAIRS]),
                             expert_i[:, :, None].broadcast_to([P, E, PAIRS]), ALU.logical_shift_right)\
                .then_inc(made_v, 1)
            ve.wait_ge(made_v, 4)
            ve.tensor_scalar(has_i[:], has_i[:], 1, None, ALU.bitwise_and)
            ve.tensor_copy(bit_f[:], bit_i[:]).then_inc(made_v, 1)
            ve.wait_ge(made_v, 5)
            ve.tensor_copy(has_f[:], has_i[:]).then_inc(made_v, 1)
            ve.wait_ge(made_v, 6)

            def row_max(b):
                ve.wait_ge(s_ready, (b + 1).number)
                ve.tensor_reduce(nmax[:, b.half, :], s_ps, X, ALU.max, negate=True).then_inc(nmax_ready, 1)

            def choose_a(b):
                if isinstance(b.quarter, int) and b.number == 0:
                    ve.wait_ge(logit_ready, 1)
                for c in range(C):
                    ins = ve.max(top[:, b.half, c, :], logit_ps[:, c, :])
                ins.then_inc(top_ready, 1)

            def choose_b(b):
                ve.wait_ge(top_ready, (b + 1).number)
                ve.tensor_tensor(shifted[:, b.half], logit_ps,
                                 top[:, b.half, :, 0:1].broadcast_to([P, C, E]), ALU.subtract)\
                    .then_inc(shifted_ready, 1)
                for c in range(C):
                    ins = ve.max_index(best[:, b.half, c, :], top[:, b.half, c, :], logit_ps[:, c, :])
                ins.then_inc(best_ready, 1)

            def choose_c(b):
                ve.wait_ge(best_ready, (b + 1).number)
                ve.tensor_tensor(onehot[:, b.slot], expert_f[:, None, None, :].broadcast_to([P, C, K, E]),
                                 best[:, b.half, :, 0:K, None].broadcast_to([P, C, K, E]),
                                 ALU.is_equal).then_inc(onehot_ready, 1)

            def choose_d(b):
                ve.wait_ge(onehot_ready, (b + 1).number)
                ve.tensor_tensor(bits[:], onehot[:, b.slot], bit_f[:, None, None, :].broadcast_to([P, C, K, E]),
                                 ALU.mult).then_inc(bits_ready, 1)

            def choose_e(b):
                ve.wait_ge(bits_ready, (b + 1).number)
                ve.tensor_reduce(code[:], bits[:].rearrange("p c k e -> p c (k e)"), X, ALU.add)\
                    .then_inc(code_ready, 1)

            def choose_f(b):
                ve.wait_ge(code_ready, (b + 1).number)
                ve.tensor_tensor(pairhot[:, b.slot], code_f[:, None, :].broadcast_to([P, C, PAIRS]),
                                 code[:, :, None].broadcast_to([P, C, PAIRS]), ALU.is_equal)\
                    .then_inc(pairhot_ready, 1)

            def place_a(b):
                ve.wait_ge(rank_ready, (b + 1).number)
                if (b + 1).valid(BATCHES):
                    ve.wait_ge(logit_ready, (b + 2).number)
                ve.tensor_tensor(picked[:], rank_ps, pairhot[:, b.slot], ALU.mult).then_inc(picked_ready, 1)

            def place_b(b):
                ve.wait_ge(picked_ready, (b + 1).number)
                ve.tensor_reduce(rank_all[:, bass.ds(b.number * C, C)], picked[:], X, ALU.add)\
                    .then_inc(ranked, 1)

            def invert_total(b):
                ve.wait_ge(expd_ready, (b + 1).number * C)
                ve.reciprocal(rtotal[:, b.slot], total[:, b.slot]).then_inc(rtotal_ready, 1)

            def residual_a(b):
                if not (b + 1).valid(BATCHES):
                    ve.wait_ge(prob_ready, BATCHES * C)
                ve.reciprocal(rinv[:, b.half], psum_[:, b.half]).then_inc(rinv_ready, 1)

            def residual(b):
                ve.wait_ge(rinv_ready, (b + 1).number)
                ve.wait_ge(o_ready, (b + 1).number)
                ve.wait_ge(x_loaded[b.slot], 16 * (b.turn + 1))
                for c in range(C):
                    ins = ve.scalar_tensor_tensor(out=hid[:, b.half, c, :], in0=o_ps[:, c, :],
                                                  scalar=rinv[:, b.half, c:c + 1],
                                                  in1=xin[:, b.slot, c, :], op0=ALU.mult, op1=ALU.add)
                ins.then_inc(hid_ready, 1)

            def statistics(b):
                ve.wait_ge(hid_ready, (b + 1).number)
                for c in range(C):
                    ve.bn_stats(stats[:, c, :], hid[:, b.half, c, :]).then_inc(stats_ready, 1)

            def aggregate(b):
                for c in range(C):
                    ve.bn_aggr(mv[:, b.half, c, :], stats[:, c, :]).then_inc(mv_ready, 1)

            def normalise(b):
                ve.wait_ge(rstd_ready, (b + 1).number)
                wait(ve, rows_stored[b.slot], b.turn * 16)
                for c in range(C):
                    ins = ve.tensor_scalar(x1[:, b.slot, c, 0:D], hid[:, b.half, c, :],
                                           mv[:, b.half, c, 0:1], rstd[:, b.half, c:c + 1],
                                           ALU.subtract, ALU.mult)
                ins.then_inc(x1_ready, 1)

            def step(i):
                old, new, routed, ranked_ = i - 2, i - 1, i - 4, i - 5
                if new.valid(BATCHES):
                    row_max(new)
                if (i - 3).valid(BATCHES):
                    normalise(i - 3)
                if old.valid(BATCHES):
                    residual_a(old)
                if ranked_.valid(BATCHES):
                    place_a(ranked_)
                if routed.valid(BATCHES):
                    choose_a(routed)
                if old.valid(BATCHES):
                    residual(old)
                if routed.valid(BATCHES):
                    choose_b(routed)
                if old.valid(BATCHES):
                    statistics(old)
                if ranked_.valid(BATCHES):
                    place_b(ranked_)
                if old.valid(BATCHES):
                    ve.wait_ge(stats_ready, (old + 1).number * C)
                if routed.valid(BATCHES):
                    choose_c(routed)
                if old.valid(BATCHES):
                    aggregate(old)
                if routed.valid(BATCHES):
                    choose_d(routed)
                if ranked_.valid(BATCHES):
                    invert_total(ranked_)
                if routed.valid(BATCHES):
                    choose_e(routed)
                    choose_f(routed)

            steps(ve, *WHOLE, LAST, step)

            made_steps = [0]

            def tabled(ins):
                made_steps[0] += 1
                ins.then_inc(table, 1)
                ve.wait_ge(table, made_steps[0])

            ve.wait_ge(count_ready, 1)
            tabled(ve.tensor_copy(count[:], bank[6][:, 0:PAIRS]))
            tabled(ve.tensor_tensor_scan(upto[:], count[:], zeros[:], 0.0, ALU.add, ALU.add))
            tabled(ve.tensor_tensor(start[:], upto[:], count[:], ALU.subtract))
            ve.sem_inc(start_ready)

            ve.wait_ge(pairs_kept, BATCHES)
            ve.wait_ge(ranked, BATCHES)
            tabled(ve.tensor_tensor(started[:, POOL_TILES:], pairhot_all[:, POOL_TILES:],
                                    start[:, None, :].broadcast_to([P, TILES - POOL_TILES, PAIRS]), ALU.mult))
            ve.wait_ge(started_ready, 1)
            tabled(ve.tensor_reduce(pos_f[:], started[:], X, ALU.add))
            tabled(ve.tensor_tensor(pos_i[:], pos_f[:], rank_all[:], ALU.add))
            ve.tensor_scalar(posblk_i[:], pos_i[:], P.bit_length() - 1, None, ALU.logical_shift_right)
            tabled(ve.tensor_scalar(posrow_i[:], pos_i[:], P - 1, None, ALU.bitwise_and))
            ve.tensor_copy(posblk[:], posblk_i[:])
            tabled(ve.tensor_copy(posrow[:], posrow_i[:]))
            for g in range(TILES // GROUP):
                wait(ve, group_done, g - 1)
                ve.tensor_tensor(blkhot[:, g % 2], item_f[:, None, 0:BLOCKS].broadcast_to([P, GROUP, BLOCKS]),
                                 posblk[:, g * GROUP:(g + 1) * GROUP, None].broadcast_to([P, GROUP, BLOCKS]),
                                 ALU.is_equal).then_inc(blkhot_ready, 1)
                ve.tensor_tensor(rowhot[:, g % 2], item_f[:, None, 0:P].broadcast_to([P, GROUP, P]),
                                 posrow[:, g * GROUP:(g + 1) * GROUP, None].broadcast_to([P, GROUP, P]),
                                 ALU.is_equal).then_inc(rowhot_ready, 1)
            tabled(ve.tensor_scalar(below[:], start[0:BLOCKS], edge_f[0:BLOCKS, 1:2], None, ALU.is_lt))
            tabled(ve.scalar_tensor_tensor(out=inside[:], in0=upto[0:BLOCKS], scalar=edge_f[0:BLOCKS, 0:1],
                                           in1=below[:], op0=ALU.is_gt, op1=ALU.mult))
            tabled(ve.tensor_tensor(among[:], has_f[0:BLOCKS], inside[:, None, :].broadcast_to([BLOCKS, E, PAIRS]),
                                    ALU.mult))
            tabled(ve.tensor_reduce(active[:], among[:], X, ALU.max))
            ve.tensor_tensor_scan(scan[:], active[:], zeros[0:BLOCKS, 0:E], 0.0, ALU.add, ALU.add)\
                .then_inc(scan_ready, 1)
            ve.wait_ge(group_done, TILES // GROUP)
            tabled(ve.tensor_copy(sorted_f[:], bank[2][:, BLOCKS:2 * BLOCKS]))
            tabled(ve.scalar_tensor_tensor(out=sorted_f[:], in0=bank[2][:, 0:BLOCKS], scalar=float(P),
                                           in1=sorted_f[:], op0=ALU.mult, op1=ALU.add))
            ve.sem_inc(sorted_ready)
            ve.wait_ge(scan_ready, 1)
            ve.wait_ge(blocks_before, 1)
            tabled(ve.tensor_tensor(cells[:], scan[:], bank[0][0:BLOCKS, 0:1].broadcast_to([BLOCKS, E]), ALU.add))
            tabled(ve.tensor_tensor(past[:], cells[:, None, :].broadcast_to([BLOCKS, ITEMS, E]),
                                    item_f[0:BLOCKS, :, None].broadcast_to([BLOCKS, ITEMS, E]), ALU.is_le))
            with nc.allow_low_precision(reason="counts up to 8"):
                ve.tensor_reduce(npast[:], past[:], X, ALU.add).then_inc(npast_ready, 1)
            ve.wait_ge(cells_ready, 1)
            tabled(ve.tensor_copy(cell_i[:], bank[1][0:1, 0:ITEMS]))
            ve.tensor_scalar(act_tab[:, 0:ITEMS], cell_i[:], E - 1, WE.bit_length() - 1,
                             ALU.bitwise_and, ALU.logical_shift_left).then_inc(items_known, 1)
            ve.tensor_scalar(exp_i[:], cell_i[:], E - 1, None, ALU.bitwise_and)
            tabled(ve.tensor_scalar(blk_i[:], cell_i[:], E.bit_length() - 1, None, ALU.logical_shift_right))
            ve.tensor_copy(pe_tab[:, 2:ITEMS + 2, 0], act_tab[:, 0:ITEMS])
            ve.tensor_scalar(pe_tab[:, 0:ITEMS, 1], blk_i[:], float(P), None, ALU.mult).then_inc(items_known, 1)
            tabled(ve.tensor_scalar(ve_tab[:, 2:ITEMS + 2, 0], blk_i[:], float(ROW), None, ALU.mult))
            tabled(ve.scalar_tensor_tensor(out=ve_tab[:, 2:ITEMS + 2, 1], in0=exp_i[:], scalar=float(D),
                                           in1=ve_tab[:, 2:ITEMS + 2, 0], op0=ALU.add, op1=ALU.add))

            def multiply(m, k):
                ve.wait_ge(act_ready, m.number * 2 + (k + 1))
                ve.tensor_tensor(gated[:, 2 * m.half + k], act1[:, k], h_ps[k][:, HC * P:2 * HC * P], ALU.mult)\
                    .then_inc(gated_ready, 1)

            def add_up(m, k, column, score):
                ve.wait_ge(y_ready, m.number * 2 + (k + 1))
                wait(ve, summed, m.number * 2 + k)
                rows = rows_flat[:, bass.ds(column, D)]
                ve.scalar_tensor_tensor(out=rows, in0=y_ps[2 * m.half + k][:, 0:D],
                                        scalar=rows_flat[:, bass.ds(score, 1)], in1=rows,
                                        op0=ALU.mult, op1=ALU.add).then_inc(summed, 1)

            def done_rows(f, width):
                if isinstance(f.quarter, int):
                    return rows_flat[:, f.number * ROW:f.number * ROW + width]
                return rows_flat[:, f.offset * ROW:][:, bass.ds(f.quarter * (4 * ROW), width)]

            def statistics2(f):
                ve.bn_stats(stats2[:, f.half, :], done_rows(f, D)).then_inc(stats2_ready, 1)

            def finish(f):
                ve.wait_ge(rstd2_ready, (f + 1).number)
                wait(ve, stored[f.slot], f.turn * 16)
                ve.tensor_scalar(res[:, f.slot, :], done_rows(f, D), mv2[:, f.slot, 0:1], rstd2[:, f.slot, :],
                                 ALU.subtract, ALU.mult).then_inc(res_ready, 1)

            def aggregate2(f):
                ve.bn_aggr(mv2[:, f.slot, :], stats2[:, f.half, :]).then_inc(mv2_ready, 1)

            items = [ve.alloc_register(f"item{k}_{what}") for k in range(4) for what in ("column", "score")]
            value = []

            def step2(m):
                f = m - DONE_LAG
                if m.valid(STEPS):
                    multiply(m, 0)
                if m.half == 0 and m.valid(STEPS + 1):
                    value[:] = load_values(ve, items, ve_tab[:].rearrange("o i j -> o (i j)")[
                        0:1, bass.ds(m.number * 4, 8)], [TOP_COLUMN, TOP_COLUMN + ROW - 1] * 4)
                for k in range(2):
                    if k == 1 and m.valid(STEPS):
                        multiply(m, 1)
                    if (m - 1).valid(STEPS):
                        add_up(m - 1, k, value[4 * m.half + 2 * k], value[4 * m.half + 2 * k + 1])
                if f.valid(BLOCKS):
                    statistics2(f)
                if (f - 1).valid(BLOCKS):
                    ve.wait_ge(stats2_ready, f.number)
                if (f - 3).valid(BLOCKS):
                    finish(f - 3)
                if (f - 1).valid(BLOCKS):
                    aggregate2(f - 1)

            steps(ve, *WHOLE2, LAST2, step2)


_INS = ["L0_attn_x", "L0_attn_W_qkv", "L0_ffn_gate_w", "L0_ffn_w1", "L0_ffn_w2", "L0_ffn_w3"]


def kernel(**inputs):
    import numpy as _np
    import concourse.bacc as _bacc
    from concourse import mybir as _mybir
    from concourse.bass_utils import run_bass_kernel_spmd as _run

    nc = _bacc.Bacc("TRN2", target_bir_lowering=False, num_devices=1)
    arrays, args = {}, []
    for name in _INS:
        a = _np.ascontiguousarray(inputs[name])
        arrays[f"in_{name}_dram"] = a
        args.append(nc.dram_tensor(f"in_{name}_dram", a.shape, _mybir.dt.from_np(a.dtype), kind="ExternalInput").ap())
    shape = inputs["L0_attn_x"].shape
    args.append(nc.dram_tensor("out_0_dram", shape, _mybir.dt.float32, kind="ExternalOutput").ap())
    attention_moe(nc, *args)
    r = _run(nc, [arrays], core_ids=[0])
    return r.results[0]["out_0_dram"]
```
